# Optimizing a Trainium2 kernel written in Bass

```python
import numpy as np
import jax
import jax.numpy as jnp

def _softmax(x, axis=-1):
    return jax.nn.softmax(x, axis=axis)

def _gelu(x):
    return jax.nn.gelu(x, approximate=True)

def _silu(x):
    return jax.nn.silu(x)

def _sigmoid(x):
    return jax.nn.sigmoid(x)

def _layernorm(x, axis=-1, eps=1e-05):
    m = jnp.mean(x, axis=axis, keepdims=True)
    v = jnp.var(x, axis=axis, keepdims=True)
    return (x - m) / jnp.sqrt(v + eps)

def _scatter_add(tgt, idx, src, axis=0):
    return tgt.at[idx].add(src)

def _segment_sum(src, seg, n):
    return jax.ops.segment_sum(src, seg, n)
kernel_name = 'mk_xattn_ffn_d1_seqx_r8_b5b2c8'

def setup_inputs(seed: int=0):
    np.random.seed(seed)
    _w = jnp.asarray

    def _rec_inputs():
        import jax
        import jax.numpy as jnp
        _rk = jax.random.key(seed)
        x = -0.0003929 + 0.9999 * jax.random.normal(jax.random.fold_in(_rk, 1), (8, 128, 512), jnp.float32)
        _lenS = 128 - jax.random.randint(jax.random.fold_in(_rk, 7), (8,), 0, max(1, 128 // 4) + 1, jnp.int32)
        _lenS2 = 128 - jax.random.randint(jax.random.fold_in(_rk, 8), (8,), 0, max(1, 128 // 4) + 1, jnp.int32)
        _ctx_4096P = jax.random.normal(jax.random.fold_in(_rk, 11), (8, 16, 512), jnp.float32)
        _ctx_4096c = jax.random.dirichlet(jax.random.fold_in(_rk, 511), 0.3 * jnp.ones((16,), jnp.float32), (8, 128))
        _ctx_4096t = jnp.einsum('bsk,bkd->bsd', _ctx_4096c, _ctx_4096P)
        _ctx_4096t = _ctx_4096t * jax.lax.rsqrt(jnp.mean(jnp.square(_ctx_4096t)) + 1e-12) * 0.953939
        ctx_4096 = 2.81802e-05 + 1.00001 * (_ctx_4096t + 0.3 * jax.random.normal(jax.random.fold_in(_rk, 611), (8, 128, 512), jnp.float32))
        pos_BxS2 = jnp.broadcast_to(jnp.arange(128, dtype=jnp.int32), (8, 128))
        _validS = jnp.arange(128)[None, :] < _lenS[:, None]
        _validS2 = jnp.arange(128)[None, :] < _lenS2[:, None]
        _causal = jnp.tril(jnp.ones((128, 128), dtype=bool))
        mask_BxSxS2_ik0 = jnp.where(jnp.broadcast_to(_validS2[:, None, :], (8, 128, 128)), 0, 1).astype(jnp.int32)
        return (x, ctx_4096, pos_BxS2, mask_BxSxS2_ik0)
    x, ctx_4096, pos_BxS2, mask_BxSxS2_ik0 = _rec_inputs()

    def _L0_xattn_setup():
        import jax, jax.numpy as jnp
        import numpy as np
        B, S, E = (2, 256, 512)
        H, KVH, D = (32, 8, 128)
        GROUPS = H // KVH
        MAX_POS = 512
        ROPE_THETA = 10000.0

        def _rope_tables(max_pos, dim, theta):
            inv_freq = 1.0 / theta ** (jnp.arange(0, dim, 2, dtype=jnp.float32) / dim)
            t = jnp.arange(max_pos, dtype=jnp.float32)
            freqs = jnp.einsum('i,j->ij', t, inv_freq)
            emb = jnp.concatenate([freqs, freqs], axis=-1)
            return (jnp.cos(emb), jnp.sin(emb))

        def _rotate_half(x):
            x1, x2 = (x[..., :x.shape[-1] // 2], x[..., x.shape[-1] // 2:])
            return jnp.concatenate([-x2, x1], axis=-1)
        key = jax.random.key(seed)
        ks = jax.random.split(key, 8)
        scale_w = 1.0 / np.sqrt(E)
        query = jax.random.normal(ks[0], (B, S, E), dtype=jnp.float32)
        k_in = jax.random.normal(ks[1], (B, S, E), dtype=jnp.float32)
        v_in = jax.random.normal(ks[2], (B, S, E), dtype=jnp.float32)
        position_ids = jnp.broadcast_to(jnp.arange(S, dtype=jnp.int64), (B, S))
        src_mask = jnp.tril(jnp.ones((S, S), dtype=jnp.int32))
        src_mask = jnp.broadcast_to(src_mask, (B, S, S))
        Wq = jax.random.normal(ks[3], (E, H * D), dtype=jnp.float32) * scale_w
        Wk = jax.random.normal(ks[4], (E, KVH * D), dtype=jnp.float32) * scale_w
        Wv = jax.random.normal(ks[5], (E, KVH * D), dtype=jnp.float32) * scale_w
        Wo = jax.random.normal(ks[6], (H * D, E), dtype=jnp.float32) * scale_w
        return {'query': query, 'key': k_in, 'value': v_in, 'position_ids': position_ids, 'src_mask': src_mask, 'Wq': Wq, 'Wk': Wk, 'Wv': Wv, 'Wo': Wo}
    _L0_xattn_all = _L0_xattn_setup()
    _L0_xattn_in = {k: v for k, v in _L0_xattn_all.items() if k in ('Wq', 'Wk', 'Wv', 'Wo')}
    del _L0_xattn_all

    def _L0_ffn_setup():
        import jax, jax.numpy as jnp
        import numpy as np
        K_TOP = 8
        key = jax.random.key(seed)
        k1, k2, k3 = jax.random.split(key, 3)
        B, S, H, E = (4, 512, 512, 64)
        hidden_states = jax.random.normal(k1, (B, S, H), dtype=jnp.float32)
        router_weight = jax.random.normal(k2, (E, H), dtype=jnp.float32)
        router_bias = jnp.zeros((E,), dtype=jnp.float32)
        expert_bias = jax.random.normal(k3, (E, H), dtype=jnp.float32) * 0.1
        return {'hidden_states': hidden_states, 'router_weight': router_weight, 'router_bias': router_bias, 'expert_bias': expert_bias}
    _L0_ffn_all = _L0_ffn_setup()
    _L0_ffn_in = {k: v for k, v in _L0_ffn_all.items() if k in ('router_weight', 'router_bias', 'expert_bias')}
    del _L0_ffn_all
    return {'x': x, 'ctx_4096': ctx_4096, 'pos_BxS2': pos_BxS2, 'mask_BxSxS2_ik0': mask_BxSxS2_ik0, 'L0_xattn_Wq': _L0_xattn_in['Wq'], 'L0_xattn_Wk': _L0_xattn_in['Wk'], 'L0_xattn_Wv': _L0_xattn_in['Wv'], 'L0_xattn_Wo': _L0_xattn_in['Wo'], 'L0_ffn_router_weight': _L0_ffn_in['router_weight'], 'L0_ffn_router_bias': _L0_ffn_in['router_bias'], 'L0_ffn_expert_bias': _L0_ffn_in['expert_bias']}

def reference(x, ctx_4096, pos_BxS2, mask_BxSxS2_ik0, L0_xattn_Wq, L0_xattn_Wk, L0_xattn_Wv, L0_xattn_Wo, L0_ffn_router_weight, L0_ffn_router_bias, L0_ffn_expert_bias):
    import jax
    import jax.numpy as jnp

    def _L0_xattn_ref(query, key, value, position_ids, src_mask, Wq, Wk, Wv, Wo):
        import jax, jax.numpy as jnp
        import numpy as np
        B, S, E = (2, 256, 512)
        H, KVH, D = (32, 8, 128)
        GROUPS = H // KVH
        MAX_POS = 512
        ROPE_THETA = 10000.0

        def _rope_tables(max_pos, dim, theta):
            inv_freq = 1.0 / theta ** (jnp.arange(0, dim, 2, dtype=jnp.float32) / dim)
            t = jnp.arange(max_pos, dtype=jnp.float32)
            freqs = jnp.einsum('i,j->ij', t, inv_freq)
            emb = jnp.concatenate([freqs, freqs], axis=-1)
            return (jnp.cos(emb), jnp.sin(emb))

        def _rotate_half(x):
            x1, x2 = (x[..., :x.shape[-1] // 2], x[..., x.shape[-1] // 2:])
            return jnp.concatenate([-x2, x1], axis=-1)
        nb, q_len, _ = query.shape
        q = (query @ Wq).reshape(nb, q_len, H, D).transpose(0, 2, 1, 3)
        k = (key @ Wk).reshape(nb, q_len, KVH, D).transpose(0, 2, 1, 3)
        v = (value @ Wv).reshape(nb, q_len, KVH, D).transpose(0, 2, 1, 3)
        cos_t, sin_t = _rope_tables(MAX_POS, D, ROPE_THETA)
        cos = cos_t[position_ids][:, None]
        sin = sin_t[position_ids][:, None]
        q = q * cos + _rotate_half(q) * sin
        k = k * cos + _rotate_half(k) * sin
        k = jnp.repeat(k, GROUPS, axis=1)
        v = jnp.repeat(v, GROUPS, axis=1)
        scores = jnp.einsum('bhqd,bhkd->bhqk', q, k) / jnp.sqrt(jnp.float32(D))
        mask = src_mask[:, None]
        scores = jnp.where(mask == 0, jnp.float32(-1000000000.0), scores)
        attn = jax.nn.softmax(scores, axis=-1)
        x = jnp.einsum('bhqk,bhkd->bhqd', attn, v)
        x = x.transpose(0, 2, 1, 3).reshape(nb, q_len, H * D)
        return x @ Wo

    def _L0_ffn_ref(hidden_states, router_weight, router_bias, expert_bias):
        import jax, jax.numpy as jnp
        import numpy as np
        K_TOP = 8
        B, S, H = hidden_states.shape
        E = router_weight.shape[0]
        T = B * S
        flat = hidden_states.reshape(T, H)
        logits = jnp.einsum('th,eh->te', flat, router_weight) + router_bias
        scores = jax.nn.softmax(logits, axis=-1)
        topk_w, topk_idx = jax.lax.top_k(scores, K_TOP)
        w_sum = topk_w.sum(axis=-1, keepdims=True)
        w_dense = jnp.zeros((T, E), dtype=scores.dtype).at[jnp.arange(T)[:, None], topk_idx].add(topk_w)
        bias_mix = jnp.einsum('te,eh->th', w_dense, expert_bias)
        out = flat * w_sum + bias_mix
        return out.reshape(B, S, H)
    x = x + _L0_xattn_ref(_layernorm(x, axis=-1), ctx_4096, ctx_4096, pos_BxS2, mask_BxSxS2_ik0, L0_xattn_Wq, L0_xattn_Wk, L0_xattn_Wv, L0_xattn_Wo)
    x = x + _L0_ffn_ref(_layernorm(x, axis=-1), L0_ffn_router_weight, L0_ffn_router_bias, L0_ffn_expert_bias)
    return x

_drawn_inputs = setup_inputs


def setup_inputs(seed=0):
    import zlib

    import numpy as np

    out = dict(_drawn_inputs(seed))
    spreads = {'L0_ffn_router_bias': (0.0, 0.1)}
    factors = {}
    for name, (base, spread) in spreads.items():
        noise = np.random.default_rng([zlib.crc32(name.encode()), seed]).standard_normal(out[name].shape)
        drawn = base * np.exp(spread * noise) if base else spread * noise
        out[name] = jnp.asarray(drawn.astype(out[name].dtype))
    for name, factor in factors.items():
        out[name] = (out[name] * factor).astype(out[name].dtype)
    return out
```

```python
from contextlib import ExitStack

import numpy as np

import concourse.bass as bass
from concourse import mybir

F32 = mybir.dt.float32
F32R = mybir.dt.float32r
BF16 = mybir.dt.bfloat16
I32 = mybir.dt.int32
ALU = mybir.AluOpType
ACT = mybir.ActivationFunctionType
X_AXIS = mybir.AxisListType.X

B, S, E = 8, 128, 512
KV, GH, D = 8, 4, 128
NX, TOP = 64, 8
MAX_POS, THETA = 512, 10000.0
EPS = 1e-5
SCALE = float(D) ** -0.5
MASKED = -(2.0**100)

P = 128
W = 512
C = E // P
T = B * S
HALF = D // 2
HB = W // S
NH = T // W
KB = KV // GH
STEPS = KV * B
QT = KV * NH * GH
AHEAD = 6

U_CTX = 0
U_TAB = U_CTX + B
U_K = U_TAB + 2 * NH
U_V = U_K + KV * (NH + 1)
U_Q = U_V + KB * B

RA, RB = 2, 4
A_Q = KV
B_V = B
B_O = B_V + KB * C


def xattn_ffn(nc, x, ctx, pos, mask, rope, wq, wk, wv, wo, router, router_bias, expert_bias, out):
    with ExitStack() as stack:
        kib = 1024
        base = -(-nc.sbuf_base // 32) * 32

        def at(name, cols, dt, offset, parts=P):
            return nc.alloc_sbuf_tensor_at(name, [parts] + cols, dt, offset=base + int(offset * kib))

        def bank(name):
            return stack.enter_context(nc.psum_tensor(name, [P, W], F32))

        def sem(name):
            return stack.enter_context(nc.semaphore(name))

        xT_hi = at("xT_hi", [C, T], F32R, 0)
        xT_lo = at("xT_lo", [C, T], F32R, 16)
        resid = at("resid", [B, E], F32, 32)
        cosT = at("cosT", [T], F32, 48)
        sinT = at("sinT", [T], F32, 52)
        mask_bias = at("mask_bias", [B, S], BF16, 56)
        kT = at("kT", [KV, T], F32, 58)
        values = at("values", [B, KV * D], F32, 90)
        table = at("table", [B, 2 * D], F32, 90)
        mask_in = at("mask_in", [B, S], I32, 98)
        x_norm = at("x_norm", [2, E], F32, 102)
        router_in = at("router_in", [E], F32, 106, NX)
        ff_x = at("ff_x", [2, E], F32, 58)
        ff_xT = at("ff_xT", [E], F32, 62)
        ff_out = at("ff_out", [2, E], F32, 64)
        ff_logit = at("ff_logit", [NX], F32, 68)
        ff_exp = at("ff_exp", [NX], F32, 68.25)
        ff_prob = at("ff_prob", [NX], F32, 68.5)
        ff_rest = at("ff_rest", [NX], F32, 68.75)
        ff_kept = at("ff_kept", [NX], F32, 69)
        ff_keptT = at("ff_keptT", [S], F32, 69.5, NX)
        wv_hi = [at("wv0_hi", [C, W], F32R, 122), at("wv1_hi", [C, W], F32R, 138)]
        wv_lo = [at("wv0_lo", [C, W], F32R, 130), at("wv1_lo", [C, W], F32R, 146)]
        wq_hi = at("wq_hi", [GH, C, D], F32R, 122)
        wq_lo = at("wq_lo", [GH, C, D], F32R, 130)
        wk_hi = at("wk_hi", [2, C, D], F32R, 138)
        wk_lo = at("wk_lo", [2, C, D], F32R, 142)
        qT = at("qT", [2, GH, W], F32, 138)
        ctxT_hi = at("ctxT_hi", [C, T], F32R, 154)
        ctxT_lo = at("ctxT_lo", [C, T], F32R, 170)
        wo_hi = at("wo_hi", [GH, E], F32R, 154)
        wo_lo = at("wo_lo", [GH, E], F32R, 162)
        probs = at("probs", [2, GH, S], F32, 170)
        pT_hi = at("pT_hi", [W], F32R, 174)
        pT_lo = at("pT_lo", [W], F32R, 176)
        oT_hi = at("oT_hi", [W], F32R, 178)
        oT_lo = at("oT_lo", [W], F32R, 180)
        v_hi = at("v_hi", [2, D], F32R, 182)
        v_lo = at("v_lo", [2, D], F32R, 183)
        ring_a = at("ring_a", [RA, W], F32, 186)
        ring_b = at("ring_b", [RB, W], F32, 190)
        rot = at("rot", [2, W], F32, 198)
        ident = at("ident", [P], F32, 202)
        routerT = at("routerT", [C, NX], F32, 202.5)
        ebias = at("ebias", [E], F32, 203.5, NX)
        rbias = at("rbias", [NX], F32, 205.5)
        pos_in = at("pos_in", [B], I32, 205.75)
        pos_wrap = at("pos_wrap", [B], F32, 205.8125)
        pos_sum = at("pos_sum", [B], F32, 205.875)
        pos_idx = at("pos_idx", [B], I32, 205.9375)
        x_stats = at("x_stats", [B, 6], F32, 206)
        x_mv = at("x_mv", [B, 2], F32, 206.1875)
        x_var = at("x_var", [B], F32, 206.25)
        x_rstd = at("x_rstd", [B], F32, 206.28125)
        power = at("power", [B], F32, 206.3125)
        negmax = at("negmax", [2, GH], F32, 206.34375)
        sums = at("sums", [2, GH], F32, 206.375)
        rsum = at("rsum", [2, GH], F32, 206.40625)
        ff_stats = at("ff_stats", [6], F32, 206.4375)
        ff_mv = at("ff_mv", [2], F32, 206.46875)
        ff_var = at("ff_var", [1], F32, 206.5)
        ff_rstd = at("ff_rstd", [1], F32, 206.53125)
        ff_negmax = at("ff_negmax", [1], F32, 206.5625)
        ff_sum = at("ff_sum", [1], F32, 206.59375)
        ff_rsum = at("ff_rsum", [1], F32, 206.625)
        ff_top = at("ff_top", [TOP], F32, 206.65625)
        ff_wsum = at("ff_wsum", [1], F32, 206.6875)
        assert base + int(206.75 * kib) <= nc.sbuf_usable_end

        proj = [bank("proj0"), bank("proj1")]
        score = [bank("score0"), bank("score1")]
        probT = bank("probT")
        attnT = bank("attnT")
        outp = [bank("outp0"), bank("outp1")]

        dma_a = [sem(f"dma_a{i}") for i in range(RA)]
        dma_b = [sem(f"dma_b{i}") for i in range(RB)]
        dma_x = sem("dma_x")
        dma_pos = sem("dma_pos")
        dma_mask = sem("dma_mask")
        dma_table = [sem(f"dma_table{i}") for i in range(B)]
        dma_router = sem("dma_router")
        dma_ffn = sem("dma_ffn")
        dma_out = [sem("dma_out0"), sem("dma_out1")]
        ident_done = sem("ident_done")
        power_done = sem("power_done")
        pos_wrapped = sem("pos_wrapped")
        pos_summed = sem("pos_summed")
        pos_done = sem("pos_done")
        x_counted = sem("x_counted")
        x_averaged = sem("x_averaged")
        var_done = sem("var_done")
        rstd_done = sem("rstd_done")
        norm_done = sem("norm_done")
        router_ps = sem("router_ps")
        router_done = sem("router_done")
        proj_done = sem("proj_done")
        proj_hi = sem("proj_hi")
        proj_free = sem("proj_free")
        rot_done = sem("rot_done")
        sin_done = sem("sin_done")
        rope_done = sem("rope_done")
        a_hi = sem("a_hi")
        a_lo = sem("a_lo")
        b_hi = sem("b_hi")
        b_lo = sem("b_lo")
        qk_done = sem("qk_done")
        masked = sem("masked")
        max_done = sem("max_done")
        exp_done = sem("exp_done")
        rsum_done = sem("rsum_done")
        soft_done = sem("soft_done")
        pt_done = sem("pt_done")
        pt_hi = sem("pt_hi")
        pt_lo = sem("pt_lo")
        vhi_done = sem("vhi_done")
        vlo_done = sem("vlo_done")
        pv_done = sem("pv_done")
        ot_hi = sem("ot_hi")
        ot_lo = sem("ot_lo")
        o_done = sem("o_done")
        acc_done = sem("acc_done")
        f_stats = sem("f_stats")
        f_mv = sem("f_mv")
        f_var = sem("f_var")
        f_rstd = sem("f_rstd")
        f_x = sem("f_x")
        f_xT = sem("f_xT")
        f_xTs = sem("f_xTs")
        f_logit = sem("f_logit")
        f_biased = sem("f_biased")
        f_max = sem("f_max")
        f_exp = sem("f_exp")
        f_rsum = sem("f_rsum")
        f_prob = sem("f_prob")
        f_top = sem("f_top")
        f_rest = sem("f_rest")
        f_kept = sem("f_kept")
        f_wsum = sem("f_wsum")
        f_keptT = sem("f_keptT")
        f_keptTs = sem("f_keptTs")
        f_mix = sem("f_mix")
        f_scaled = sem("f_scaled")
        f_mixed = sem("f_mixed")
        f_out = sem("f_out")

        block = stack.enter_context(nc.Block())

        def wait_ring(eng, sems, r, ring):
            r0, g, per = r if isinstance(r, tuple) else (r, 0, 0)
            eng.wait_ge(sems[r0 % ring], 16 * (r0 // ring + 1) + g * (16 * per // ring))

        def heads(tile):
            return tile.rearrange("p (h k) -> p h k", h=GH)

        def chunks(tile):
            return tile.rearrange("p (c k) -> p c k", c=C)

        @block.sync
        def _(sp):
            def load_wo(g, h):
                sp.wait_ge(b_lo, B_O - B_V - RB + h + 1 + g * GH)
                sp.dma_start(ring_b[:, h, :], wo[bass.ds(g * (GH * D) + h * D, D), :]).then_inc(dma_b[h % RB], 16)

            def load_wq(g, h):
                sp.wait_ge(a_lo, A_Q - RA + h + 1 + g * GH)
                sp.dma_start(ring_a[:, h % RA, :], wq[bass.ds(g * (GH * P) + h * P, P), :]).then_inc(dma_a[h % RA], 16)

            sp.dma_start(pos_in[:, :], pos).then_inc(dma_pos, 16)
            for b in range(RB):
                sp.dma_start(ring_b[:, b, :], ctx[b]).then_inc(dma_b[b], 16)
            for r in range(RA):
                sp.dma_start(ring_a[:, r, :], wk[r]).then_inc(dma_a[r], 16)
            for b in range(RB, B):
                sp.wait_ge(proj_done, U_CTX + b - RB + 1)
                sp.dma_start(ring_b[:, b % RB, :], ctx[b]).then_inc(dma_b[b % RB], 16)

            def load_wv(i):
                r = B_V + i
                half, c = i // C, i % C
                sp.dma_start(ring_b[:, r % RB, :], wv[c * P:(c + 1) * P, half * W:(half + 1) * W]).then_inc(dma_b[r % RB], 16)

            for i in range(RB):
                sp.wait_ge(proj_done, U_CTX + B - RB + i + 1)
                load_wv(i)
            for r in range(RA, KV):
                sp.wait_ge(a_lo, r - RA + 1)
                sp.dma_start(ring_a[:, r % RA, :], wk[r]).then_inc(dma_a[r % RA], 16)
            for i in range(RB, KB * C):
                sp.wait_ge(b_lo, i - RB + 1)
                load_wv(i)
            load_wq(0, 0)
            load_wq(0, 1)
            for h in range(GH):
                load_wo(0, h)
            load_wq(0, 2)
            load_wq(0, 3)
            load_wq(1, 0)
            load_wq(1, 1)

            def stream(g):
                for h in range(GH):
                    load_wo(g + 1, h)
                load_wq(g + 1, 2)
                load_wq(g + 1, 3)

            with sp.Fori(0, KV - 2) as g:
                stream(g)
                load_wq(g + 2, 0)
                load_wq(g + 2, 1)
            stream(KV - 2)
            for b in range(B):
                sp.wait_ge(f_out, b + 1)
                sp.dma_start(out[b], ff_out[:, b % 2, :]).then_inc(dma_out[b % 2], 16)
            for stored in dma_out:
                sp.wait_ge(stored, 16 * B // 2)

        @block.gpsimd
        def _(pool):
            def rotate(k, half):
                k0, g, per = k
                pool.wait_ge(rot_done, k0 + 1 + g * per)
                pool.tensor_tensor(rot[:, k0 % 2, :], rot[:, k0 % 2, :], sinT[:, half * W:(half + 1) * W],
                                   ALU.mult).then_inc(sin_done, 1)

            def lo_a(dst, hi, slot, count):
                pool.wait_ge(a_hi, count)
                pool.tensor_tensor(dst, chunks(ring_a[:, slot, :]), hi.bitcast(F32), ALU.subtract).then_inc(a_lo, 1)

            def lo_b(dst, hi, slot, count):
                pool.wait_ge(b_hi, count)
                pool.tensor_tensor(dst, ring_b[:, slot, :], hi.bitcast(F32), ALU.subtract).then_inc(b_lo, 1)

            pool.memset(ident[:, :], 0.0).then_inc(ident_done, 1)
            pool.memset(power[:, :], -0.5).then_inc(power_done, 1)
            pool.wait_ge(ident_done, 1)
            pool.affine_select(out=ident[:, :], in_=ident[:, :], compare_op=ALU.not_equal, fill=1.0, base=0,
                               pattern=[[-1, P]], channel_multiplier=1).then_inc(ident_done, 1)
            pool.wait_ge(pos_done, 1)
            for b in range(B):
                pool.indirect_dma_start(table[:, b, :], None, rope,
                                        bass.IndirectOffsetOnAxis(ap=pos_idx[:, b:b + 1], axis=0),
                                        bounds_check=MAX_POS - 1).then_inc(dma_table[b], 16)
            for g in range(2):
                lo_a(wk_lo[:, g % 2], wk_hi[:, g % 2], g % RA, g + 1)
            for g in range(KV):
                if g == 1:
                    pool.wait_ge(power_done, 1)
                    pool.wait_ge(var_done, 1)
                    pool.tensor_tensor(x_rstd[:, :], x_var[:, :], power[:, :], ALU.pow).then_inc(rstd_done, 1)
                for half in range(NH):
                    if g == 0 and half == 0:
                        pool.wait_ge(proj_free, U_TAB + 2 * NH)
                    rotate((g * NH + half, 0, 0), half)
                if g + 2 < KV:
                    lo_a(wk_lo[:, g % 2], wk_hi[:, g % 2], g % RA, g + 3)
                if g >= KV - C:
                    i = g - (KV - C)
                    lo_b(wv_lo[0][:, i, :], wv_hi[0][:, i, :], (B_V + i) % RB, i + 1)
            for i in range(C, 2 * C):
                lo_b(wv_lo[1][:, i - C, :], wv_hi[1][:, i - C, :], (B_V + i) % RB, i + 1)
            for h in range(GH):
                lo_a(wq_lo[:, h], wq_hi[:, h], h % RA, A_Q + h + 1)

            def soften(p, count):
                pool.wait_ge(rsum_done, count)
                pool.tensor_tensor(probs[:, p], probs[:, p], rsum[:, p, :].unsqueeze(2).broadcast_to([P, GH, S]),
                                   ALU.mult).then_inc(soft_done, 1)

            for j in range(AHEAD - 1):
                rotate((KV * NH + j, 0, 0), j // GH % NH)
            soften(0, 1)

            def step(g, b, last=False):
                if not (last and b + AHEAD - 1 >= B):
                    rotate((KV * NH + AHEAD - 1 + b, g, B), (b + AHEAD - 1) // GH % NH)
                if b == 0:
                    for h in range(2):
                        lo_b(wo_lo[:, h, :], wo_hi[:, h, :], h, KB * C + h + 1 + g * GH)
                if 1 <= b <= GH and not last:
                    h = b - 1
                    lo_a(wq_lo[:, h], wq_hi[:, h], h % RA, A_Q + GH + h + 1 + g * GH)
                if not (last and b == B - 1):
                    soften((b + 1) % 2, b + 2 + g * B)
                if b == 0:
                    for h in range(2, GH):
                        lo_b(wo_lo[:, h, :], wo_hi[:, h, :], h, KB * C + h + 1 + g * GH)
                if last and b >= 1:
                    ffn_rstd(b - 1)

            def ffn_rstd(b):
                pool.wait_ge(f_var, b + 1)
                pool.tensor_tensor(ff_rstd[:, :], ff_var[:, :], power[:, 0:1], ALU.pow).then_inc(f_rstd, 1)

            with pool.Fori(0, KV - 1) as g:
                for b in range(B):
                    step(g, b)
            for b in range(B):
                step(KV - 1, b, last=True)
            ffn_rstd(B - 1)

        @block.scalar
        def _(act):
            def swap_halves(u, k, done_before=True):
                u0, k0, g, per = u[0], k, u[1], u[2]
                act.wait_ge(proj_done, u0 + 1 + g * per)
                if k0 >= 2:
                    act.wait_ge(rope_done, k0 - 1 + g * per)
                act.activation(rot[0:HALF, k0 % 2, :], proj[u0 % 2][HALF:P, :], ACT.Copy)
                act.activation(rot[HALF:P, k0 % 2, :], proj[u0 % 2][0:HALF, :], ACT.Copy).then_inc(rot_done, 1)

            def hi_a(dst, slot):
                act.activation(dst, chunks(ring_a[:, slot, :]), ACT.Copy).then_inc(a_hi, 1)

            def hi_b(dst, slot):
                act.activation(dst, ring_b[:, slot, :], ACT.Copy).then_inc(b_hi, 1)

            def hi_transposed(u, dst):
                act.wait_ge(proj_done, u + 1)
                act.activation(dst, chunks(proj[u % 2][:, :]), ACT.Copy).then_inc(proj_hi, 1)

            for b in range(B):
                act.dma_start(resid[:, b, :], x[b]).then_inc(dma_x, 16)
            act.dma_start(mask_in[:, :, :], mask).then_inc(dma_mask, 16)
            act.dma_start(router_in[:, :], router).then_inc(dma_router, 16)
            act.dma_start(ebias[:, :], expert_bias).then_inc(dma_ffn, 16)
            act.dma_start(rbias[:, :], router_bias.partition_broadcast(P)).then_inc(dma_ffn, 16)
            for b in range(B):
                hi_transposed(U_CTX + b, ctxT_hi[:, :, b * S:(b + 1) * S])
            for g in range(2):
                wait_ring(act, dma_a, g, RA)
                hi_a(wk_hi[:, g % 2], g % RA)
            for g in range(KV):
                u = U_K + g * (NH + 1)
                for half in range(NH):
                    swap_halves((u + half, 0, 0), g * NH + half)
                if g + 2 < KV:
                    wait_ring(act, dma_a, g + 2, RA)
                    hi_a(wk_hi[:, g % 2], g % RA)
                hi_transposed(u + NH, xT_hi[:, :, g * S:(g + 1) * S])
                if g >= KV - C:
                    i = g - (KV - C)
                    wait_ring(act, dma_b, B_V + i, RB)
                    hi_b(wv_hi[0][:, i, :], (B_V + i) % RB)
            for i in range(C, 2 * C):
                wait_ring(act, dma_b, B_V + i, RB)
                hi_b(wv_hi[1][:, i - C, :], (B_V + i) % RB)
            act.wait_ge(proj_done, U_V + B)
            for h in range(GH):
                wait_ring(act, dma_a, A_Q + h, RA)
                hi_a(wq_hi[:, h], h % RA)

            def exps(p, count, first):
                act.wait_ge(max_done, count)
                if not first:
                    act.wait_ge(pt_done, count - 2)
                for h in range(GH):
                    last = act.activation(probs[:, p, h, :], heads(score[p][:, :])[:, h, :], ACT.Exp,
                                          bias=negmax[:, p, h:h + 1], accum_out=sums[:, p, h:h + 1])
                last.then_inc(exp_done, 1)

            for j in range(AHEAD - 1):
                if j == GH:
                    exps(0, 1, True)
                swap_halves((U_Q + j, 0, 0), KV * NH + j)

            def step(g, b, first=False, last=False):
                n = b + g * B
                if not (last and b + AHEAD - 1 >= B):
                    swap_halves((U_Q + AHEAD - 1 + b, g, B), KV * NH + AHEAD - 1 + b)
                if not (first and b < 2):
                    act.wait_ge(pv_done, n - 1)
                act.activation(v_hi[:, b % 2, :], values[:, b, bass.ds(g * D, D)], ACT.Copy).then_inc(vhi_done, 1)
                act.wait_ge(pt_done, n + 1)
                if not (first and b == 0):
                    act.wait_ge(pv_done, n)
                act.activation(pT_hi[:, :], probT[:, :], ACT.Copy).then_inc(pt_hi, 1)

                def hi_wo(h):
                    wait_ring(act, dma_b, (B_O + h, g, GH), RB)
                    if not first:
                        act.wait_ge(o_done, n * GH - GH + h + 1)
                    hi_b(wo_hi[:, h, :], h)

                if b == 0:
                    hi_wo(0)
                    hi_wo(1)
                if 1 <= b <= GH and not last:
                    h = b - 1
                    wait_ring(act, dma_a, (A_Q + GH + h, g, GH), RA)
                    act.wait_ge(proj_done, U_Q + GH + h + 1 + g * B)
                    hi_a(wq_hi[:, h], h % RA)
                if not (last and b == B - 1):
                    exps((b + 1) % 2, n + 2, first and b < 1)
                if b == 0:
                    hi_wo(2)
                    hi_wo(3)
                act.wait_ge(pv_done, n + 1)
                if not (first and b == 0):
                    act.wait_ge(o_done, n * GH)
                act.activation(oT_hi[:, :], attnT[:, :], ACT.Copy).then_inc(ot_hi, 1)
                if last:
                    ffn(b)

            def ffn(b):
                if 3 <= b < B + 3:
                    ffn_kept(b - 3)
                if 1 <= b < B + 1:
                    ffn_xT(b - 1)
                if 2 <= b < B + 2:
                    ffn_exp(b - 2)

            def ffn_xT(b):
                act.wait_ge(f_xT, b + 1)
                if b >= 1:
                    act.wait_ge(f_logit, b)
                act.activation(ff_xT[:, :], proj[0][:, :], ACT.Copy).then_inc(f_xTs, 1)

            def ffn_exp(b):
                act.wait_ge(f_max, b + 1)
                if b >= 1:
                    act.wait_ge(f_prob, b)
                act.activation(ff_exp[:, :], ff_logit[:, :], ACT.Exp, bias=ff_negmax[:, :],
                               accum_out=ff_sum[:, :]).then_inc(f_exp, 1)

            def ffn_kept(b):
                act.wait_ge(f_keptT, b + 1)
                if b >= 1:
                    act.wait_ge(f_mix, b)
                act.activation(ff_keptT[:, :], proj[1][0:NX, 0:S], ACT.Copy).then_inc(f_keptTs, 1)

            for b in range(B):
                step(0, b, first=True)
            with act.Fori(1, KV - 1) as g:
                for b in range(B):
                    step(g, b)
            for b in range(B):
                step(KV - 1, b, last=True)
            for b in range(B, B + 3):
                ffn(b)

        @block.vector
        def _(dve):
            def lo_transposed(u, hi, dst, count):
                dve.wait_ge(proj_hi, count)
                dve.tensor_tensor(dst, chunks(proj[u % 2][:, :]), hi.bitcast(F32), ALU.subtract).then_inc(proj_free, 1)

            def times_cos(u, k, g, per, dst, half):
                dve.wait_ge(rot_done, k + 1 + g * per)
                dve.tensor_tensor(dst, proj[u % 2][:, :], cosT[:, half * W:(half + 1) * W],
                                  ALU.mult).then_inc(proj_free, 1)

            def add_rotated(u, k, g, per, dst):
                dve.wait_ge(sin_done, k + 1 + g * per)
                dve.wait_ge(proj_free, u + 1 + g * per)
                dve.tensor_tensor(dst, dst, rot[:, k % 2, :], ALU.add).then_inc(rope_done, 1)

            dve.wait_ge(dma_pos, 16)
            dve.tensor_scalar(pos_wrap[:, :], pos_in[:, :], 0.0, float(MAX_POS), ALU.is_lt, ALU.mult).then_inc(pos_wrapped, 1)
            dve.wait_ge(pos_wrapped, 1)
            dve.tensor_tensor(pos_sum[:, :], pos_in[:, :], pos_wrap[:, :], ALU.add).then_inc(pos_summed, 1)
            dve.wait_ge(pos_summed, 1)
            dve.tensor_scalar(pos_idx[:, :], pos_sum[:, :], 0.0, float(MAX_POS - 1), ALU.max, ALU.min).then_inc(pos_done, 1)
            for b in range(B):
                lo_transposed(U_CTX + b, ctxT_hi[:, :, b * S:(b + 1) * S], ctxT_lo[:, :, b * S:(b + 1) * S], b + 1)
            for i in range(2 * NH):
                u = U_TAB + i
                dve.wait_ge(proj_done, u + 1)
                dst = (cosT, sinT)[i // NH]
                dve.tensor_copy(dst[:, i % NH * W:(i % NH + 1) * W], proj[u % 2][:, :]).then_inc(proj_free, 1)
            dve.wait_ge(router_ps, 1)
            dve.tensor_copy(routerT[:, :, :], score[0][:, 0:C * NX].rearrange("p (c k) -> p c k", c=C)).then_inc(router_done, 1)
            dve.wait_ge(dma_mask, 16)
            dve.tensor_scalar(mask_bias[:, :, :], mask_in[:, :, :], 0.0, MASKED, ALU.is_equal, ALU.mult).then_inc(router_done, 1)
            dve.wait_ge(dma_x, 16 * B)

            for g in range(KV):
                u = U_K + g * (NH + 1)
                if g == 0:
                    for b in range(B):
                        dve.bn_stats(x_stats[:, b, :], resid[:, b, :]).then_inc(x_counted, 1)
                    dve.wait_ge(x_counted, B)
                    for b in range(B):
                        dve.bn_aggr(x_mv[:, b, :], x_stats[:, b, :]).then_inc(x_averaged, 1)
                    dve.wait_ge(x_averaged, B)
                    dve.tensor_scalar(x_var[:, :], x_mv[:, :, 1], EPS, None, ALU.add).then_inc(var_done, 1)
                if g == 0:
                    dve.wait_ge(rstd_done, 1)
                if g >= 2:
                    dve.wait_ge(proj_done, U_K + (g - 2) * (NH + 1) + NH + 1)
                dve.tensor_scalar(x_norm[:, g % 2, :], resid[:, g, :], x_mv[:, g, 0:1], x_rstd[:, g:g + 1],
                                  ALU.subtract, ALU.mult).then_inc(norm_done, 1)
                for half in range(NH):
                    k = g * NH + half
                    dst = kT[:, g, half * W:(half + 1) * W]
                    times_cos(u + half, k, 0, 0, dst, half)
                    add_rotated(u + half, k, 0, 0, dst)
                lo_transposed(u + NH, xT_hi[:, :, g * S:(g + 1) * S], xT_lo[:, :, g * S:(g + 1) * S], B + g + 1)
            for i in range(KB * B):
                u = U_V + i
                dve.wait_ge(proj_done, u + 1)
                half, b = i // B, i % B
                dve.tensor_copy(values[:, b, half * W:(half + 1) * W], proj[u % 2][:, :]).then_inc(proj_free, 1)

            def rope_query(b0, g, part):
                j = b0
                half = j // GH
                dst = qT[:, half % 2, j % GH, :]
                if part == 0:
                    times_cos(U_Q + j, KV * NH + j, g, B, dst, half % NH)
                else:
                    add_rotated(U_Q + j, KV * NH + j, g, B, dst)

            def mask_scores(p, b, count):
                dve.wait_ge(qk_done, count)
                dve.scalar_tensor_tensor(heads(score[p][:, :]), heads(score[p][:, :]), SCALE,
                                         mask_bias[:, b, :].unsqueeze(1).broadcast_to([P, GH, S]),
                                         ALU.mult, ALU.add).then_inc(masked, 1)

            def row_max(p, count, first):
                dve.wait_ge(masked, count)
                if not first:
                    dve.wait_ge(exp_done, count - 2)
                dve.tensor_reduce(negmax[:, p, :], heads(score[p][:, :]), X_AXIS, ALU.max, negate=True).then_inc(max_done, 1)

            def invert_sums(p, count, first):
                dve.wait_ge(exp_done, count)
                if not first:
                    dve.wait_ge(soft_done, count - 2)
                dve.reciprocal(rsum[:, p, :], sums[:, p, :]).then_inc(rsum_done, 1)

            for j in range(GH):
                rope_query(j, 0, 0)
                rope_query(j, 0, 1)
            mask_scores(0, 0, 1)
            row_max(0, 1, True)
            rope_query(GH, 0, 0)
            rope_query(GH, 0, 1)
            invert_sums(0, 1, True)

            def accumulate(b, count, first):
                dve.wait_ge(o_done, count * GH)
                if not first:
                    dve.wait_ge(acc_done, count - B)
                dve.tensor_tensor(resid[:, b, :], resid[:, b, :], outp[b % 2][:, :], ALU.add).then_inc(acc_done, 1)

            def step(g, b, first=False, last=False):
                n = b + g * B
                if not (last and b == B - 1):
                    mask_scores((b + 1) % 2, (b + 1) % B, n + 2)
                query = not (last and b + AHEAD - 1 >= B)
                if query:
                    if not (first and b + AHEAD - 1 < 2 * GH):
                        dve.wait_ge(qk_done, ((b + AHEAD - 1) // GH - 1) * GH + g * B)
                    rope_query(b + AHEAD - 1, g, 0)
                dve.wait_ge(vhi_done, n + 1)
                if not (first and b < 2):
                    dve.wait_ge(pv_done, n - 1)
                dve.tensor_tensor(v_lo[:, b % 2, :], values[:, b, bass.ds(g * D, D)], v_hi[:, b % 2, :].bitcast(F32),
                                  ALU.subtract).then_inc(vlo_done, 1)
                dve.wait_ge(pt_hi, n + 1)
                if not (first and b == 0):
                    dve.wait_ge(pv_done, n)
                dve.tensor_tensor(pT_lo[:, :], probT[:, :], pT_hi[:, :].bitcast(F32), ALU.subtract).then_inc(pt_lo, 1)
                if not (last and b == B - 1):
                    row_max((b + 1) % 2, n + 2, first and b == 0)
                if query:
                    rope_query(b + AHEAD - 1, g, 1)
                if not (first and b == 0):
                    accumulate((b - 1) % B, n, first)
                if not (last and b == B - 1):
                    invert_sums((b + 1) % 2, n + 2, first and b == 0)
                dve.wait_ge(ot_hi, n + 1)
                if not (first and b == 0):
                    dve.wait_ge(o_done, n * GH)
                dve.tensor_tensor(oT_lo[:, :], attnT[:, :], oT_hi[:, :].bitcast(F32), ALU.subtract).then_inc(ot_lo, 1)
                if last:
                    ffn(b)

            def ffn(b):
                if 3 <= b < B + 3:
                    ffn_out(b - 3)
                if 1 <= b < B + 1:
                    ffn_norm(b - 1)
                if 2 <= b < B + 2:
                    ffn_route(b - 2)

            def ffn_norm(b):
                dve.wait_ge(acc_done, B * (KV - 1) + b + 1)
                dve.bn_stats(ff_stats[:, :], resid[:, b, :]).then_inc(f_stats, 1)
                dve.wait_ge(f_stats, b + 1)
                dve.bn_aggr(ff_mv[:, :], ff_stats[:, :]).then_inc(f_mv, 1)
                dve.wait_ge(f_mv, b + 1)
                dve.tensor_scalar(ff_var[:, :], ff_mv[:, 1:2], EPS, None, ALU.add).then_inc(f_var, 1)
                dve.wait_ge(f_rstd, b + 1)
                if b >= 2:
                    dve.wait_ge(f_xT, b - 1)
                    dve.wait_ge(f_scaled, b - 1)
                dve.tensor_scalar(ff_x[:, b % 2, :], resid[:, b, :], ff_mv[:, 0:1], ff_rstd[:, :],
                                  ALU.subtract, ALU.mult).then_inc(f_x, 1)

            def ffn_route(b):
                dve.wait_ge(f_logit, b + 1)
                if b == 0:
                    dve.wait_ge(dma_ffn, 32)
                else:
                    dve.wait_ge(f_exp, b)
                dve.tensor_tensor(ff_logit[:, :], proj[0][:, 0:NX], rbias[:, :], ALU.add).then_inc(f_biased, 1)
                dve.wait_ge(f_biased, b + 1)
                dve.tensor_reduce(ff_negmax[:, :], ff_logit[:, :], X_AXIS, ALU.max, negate=True).then_inc(f_max, 1)
                dve.wait_ge(f_exp, b + 1)
                dve.reciprocal(ff_rsum[:, :], ff_sum[:, :]).then_inc(f_rsum, 1)
                dve.wait_ge(f_rsum, b + 1)
                dve.tensor_scalar(ff_prob[:, :], ff_exp[:, :], ff_rsum[:, :], None, ALU.mult).then_inc(f_prob, 1)
                dve.wait_ge(f_prob, b + 1)
                dve.max(ff_top[:, :], ff_prob[:, :]).then_inc(f_top, 1)
                dve.wait_ge(f_top, b + 1)
                dve.match_replace(ff_rest[:, :], ff_top[:, :], ff_prob[:, :], 0.0).then_inc(f_rest, 1)
                dve.tensor_reduce(ff_wsum[:, :], ff_top[:, :], X_AXIS, ALU.add).then_inc(f_wsum, 1)
                dve.wait_ge(f_rest, b + 1)
                if b >= 1:
                    dve.wait_ge(f_keptT, b)
                dve.tensor_tensor(ff_kept[:, :], ff_prob[:, :], ff_rest[:, :], ALU.subtract).then_inc(f_kept, 1)
                dve.wait_ge(f_wsum, b + 1)
                dve.tensor_scalar(ff_x[:, b % 2, :], ff_x[:, b % 2, :], ff_wsum[:, :], None, ALU.mult).then_inc(f_scaled, 1)

            def ffn_out(b):
                dve.wait_ge(f_mix, b + 1)
                dve.wait_ge(f_scaled, b + 1)
                if b >= 2:
                    dve.wait_ge(dma_out[b % 2], 16 * (b // 2))
                dve.tensor_tensor(ff_out[:, b % 2, :], proj[1][:, :], ff_x[:, b % 2, :], ALU.add).then_inc(f_mixed, 1)
                dve.wait_ge(f_mixed, b + 1)
                dve.tensor_tensor(ff_out[:, b % 2, :], ff_out[:, b % 2, :], resid[:, b, :], ALU.add).then_inc(f_out, 1)

            for b in range(B):
                step(0, b, first=True)
            with dve.Fori(1, KV - 1) as g:
                for b in range(B):
                    step(g, b)
            for b in range(B):
                step(KV - 1, b, last=True)
            accumulate(B - 1, STEPS, False)
            for b in range(B, B + 3):
                ffn(b)

        @block.tensor
        def _(pe):
            def three(ps, pairs):
                for i, (s_hi, s_lo, m_hi, m_lo) in enumerate(pairs):
                    pe.matmul(ps, s_hi, m_hi, start=i == 0, stop=False)
                    pe.matmul(ps, s_hi, m_lo, start=False, stop=False)
                    last = pe.matmul(ps, s_lo, m_hi, start=False, stop=i == len(pairs) - 1)
                return last

            def bank_free(u):
                if u >= 2:
                    pe.wait_ge(proj_free, u - 1)

            def transposed(u, tile):
                bank_free(u)
                for c in range(C):
                    last = pe.transpose(proj[u % 2][:, c * P:(c + 1) * P], tile[c], ident[:, :])
                last.then_inc(proj_done, 1)

            pe.wait_ge(ident_done, 2)
            for b in range(B):
                wait_ring(pe, dma_b, b, RB)
                transposed(U_CTX + b, [ring_b[:, b % RB, c * P:(c + 1) * P] for c in range(C)])
            for b in range(B):
                pe.wait_ge(dma_table[b], 16)
            for i in range(2 * NH):
                kind, half = i // NH, i % NH
                transposed(U_TAB + i, [table[:, half * HB + b, kind * D:(kind + 1) * D] for b in range(HB)])
            pe.wait_ge(dma_router, 16)
            for c in range(C):
                last = pe.transpose(score[0][:, c * NX:(c + 1) * NX], router_in[:, c * P:(c + 1) * P], ident[0:NX, 0:NX])
            last.then_inc(router_ps, 1)
            for g in range(KV):
                pe.wait_ge(a_lo, g + 1)
                for half in range(NH):
                    u = U_K + g * (NH + 1) + half
                    bank_free(u)
                    cols = slice(half * W, (half + 1) * W)
                    three(proj[u % 2][:, :], [(wk_hi[:, g % 2, c, :], wk_lo[:, g % 2, c, :],
                                               ctxT_hi[:, c, cols], ctxT_lo[:, c, cols]) for c in range(C)]).then_inc(proj_done, 1)
                pe.wait_ge(norm_done, g + 1)
                transposed(U_K + g * (NH + 1) + NH, [x_norm[:, g % 2, c * P:(c + 1) * P] for c in range(C)])
            for i in range(KB * B):
                half, b = i // B, i % B
                if b == 0:
                    pe.wait_ge(b_lo, (half + 1) * C)
                u = U_V + i
                bank_free(u)
                rows = slice(b * S, (b + 1) * S)
                three(proj[u % 2][:, :], [(ctxT_hi[:, c, rows], ctxT_lo[:, c, rows],
                                           wv_hi[half][:, c, :], wv_lo[half][:, c, :]) for c in range(C)]).then_inc(proj_done, 1)

            def project_query(b0, g):
                h, half = b0 % GH, b0 // GH % NH
                if half == 0:
                    pe.wait_ge(a_lo, A_Q + b0 // B * GH + h + 1 + g * GH)
                pe.wait_ge(proj_free, U_Q + b0 - 1 + g * B)
                cols = slice(half * W, (half + 1) * W)
                three(proj[b0 % 2][:, :], [(wq_hi[:, h, c, :], wq_lo[:, h, c, :],
                                            xT_hi[:, c, cols], xT_lo[:, c, cols]) for c in range(C)]).then_inc(proj_done, 1)

            def scores(b0, g, first):
                p, b = b0 % 2, b0 % B
                half = b0 // HB
                pe.wait_ge(rope_done, KV * NH + (half + 1) * GH + g * B)
                if not first:
                    pe.wait_ge(exp_done, b0 - 1 + g * B)
                for h in range(GH):
                    last = pe.matmul(score[p][:, h * S:(h + 1) * S], qT[:, half % 2, h, b % HB * S:(b % HB + 1) * S],
                                     kT[:, b0 // B + g, b * S:(b + 1) * S], start=True, stop=True)
                last.then_inc(qk_done, 1)

            def step(g, b, first=False, last=False):
                n = b + g * B
                if not (last and b == B - 1):
                    scores(b + 1, g, first and b == 0)
                pe.wait_ge(soft_done, n + 1)
                if not (first and b == 0):
                    pe.wait_ge(pt_lo, n)
                for h in range(GH):
                    ins = pe.transpose(probT[:, h * S:(h + 1) * S], probs[:, b % 2, h, :], ident[:, :])
                ins.then_inc(pt_done, 1)
                if not (first and b == 0):
                    output((b - 1) % B, n - 1, first and b < 3, b == 1, g)
                pe.wait_ge(pt_lo, n + 1)
                pe.wait_ge(vlo_done, n + 1)
                if not (first and b == 0):
                    pe.wait_ge(ot_lo, n)
                three(attnT[:, :], [(v_hi[:, b % 2, :], v_lo[:, b % 2, :], pT_hi[:, :], pT_lo[:, :])]).then_inc(pv_done, 1)
                if not (last and b + AHEAD >= B):
                    project_query(b + AHEAD, g)
                if last:
                    ffn(b)

            def output(b, n, first, fresh, g):
                pe.wait_ge(ot_lo, n + 1)
                if not first:
                    pe.wait_ge(acc_done, n - 1)
                for h in range(GH):
                    if fresh:
                        pe.wait_ge(b_lo, KB * C + h + 1 + g * GH)
                    cols = slice(h * S, (h + 1) * S)
                    w = (wo_hi[:, h, :], wo_lo[:, h, :])
                    pe.matmul(outp[b % 2][:, :], oT_hi[:, cols], w[0], start=h == 0, stop=False)
                    pe.matmul(outp[b % 2][:, :], oT_hi[:, cols], w[1], start=False, stop=False)
                    pe.matmul(outp[b % 2][:, :], oT_lo[:, cols], w[0], start=False, stop=h == GH - 1).then_inc(o_done, 1)

            def ffn(b):
                if 3 <= b < B + 3:
                    ffn_mix(b - 3)
                if 1 <= b < B + 1:
                    ffn_logits(b - 1)
                if 2 <= b < B + 2:
                    ffn_kept(b - 2)

            def ffn_logits(b):
                pe.wait_ge(f_x, b + 1)
                if b == 0:
                    pe.wait_ge(proj_free, U_Q + QT - 1)
                else:
                    pe.wait_ge(f_biased, b)
                for c in range(C):
                    last = pe.transpose(proj[0][:, c * P:(c + 1) * P], ff_x[:, b % 2, c * P:(c + 1) * P], ident[:, :])
                last.then_inc(f_xT, 1)
                pe.wait_ge(f_xTs, b + 1)
                for c in range(C):
                    last = pe.matmul(proj[0][:, 0:NX], ff_xT[:, c * P:(c + 1) * P], routerT[:, c, :],
                                     start=c == 0, stop=c == C - 1)
                last.then_inc(f_logit, 1)

            def ffn_kept(b):
                pe.wait_ge(f_kept, b + 1)
                if b == 0:
                    pe.wait_ge(proj_free, U_Q + QT)
                else:
                    pe.wait_ge(f_mixed, b)
                pe.transpose(proj[1][0:NX, 0:S], ff_kept[:, :], ident[:, :]).then_inc(f_keptT, 1)

            def ffn_mix(b):
                pe.wait_ge(f_keptTs, b + 1)
                if b == 0:
                    pe.wait_ge(dma_ffn, 32)
                pe.matmul(proj[1][:, :], ff_keptT[:, :], ebias[:, :], start=True, stop=True).then_inc(f_mix, 1)

            for j in range(AHEAD):
                if j == AHEAD - 1:
                    pe.wait_ge(router_done, 2)
                    scores(0, 0, True)
                if j == GH:
                    project_query(j, 0)
                else:
                    project_query(j, 0)
            for b in range(B):
                step(0, b, first=True)
            with pe.Fori(1, KV - 1) as g:
                for b in range(B):
                    step(g, b)
            for b in range(B):
                step(KV - 1, b, last=True)
            output(B - 1, STEPS - 1, False, False, KV - 1)
            for b in range(B, B + 3):
                ffn(b)


def rope_table():
    inv = (np.float32(1.0) / np.float32(THETA) ** (np.arange(0, D, 2, dtype=np.float32) / np.float32(D))).astype(np.float32)
    angle = np.arange(MAX_POS, dtype=np.float32)[:, None] * inv[None, :]
    cos, sin = np.cos(angle), np.sin(angle)
    return np.concatenate([cos, cos, -sin, sin], axis=1).astype(np.float32)


def kernel(x, ctx_4096, pos_BxS2, mask_BxSxS2_ik0, L0_xattn_Wq, L0_xattn_Wk, L0_xattn_Wv, L0_xattn_Wo,
           L0_ffn_router_weight, L0_ffn_router_bias, L0_ffn_expert_bias):
    import concourse.bacc as bacc
    from concourse.bass_utils import run_bass_kernel_spmd

    def tiled(w, n):
        return w.reshape(C, P, n, D).transpose(2, 1, 0, 3).reshape(n, P, C * D)

    arrays = {
        "x": x,
        "ctx": ctx_4096,
        "pos": np.asarray(pos_BxS2).T,
        "mask": np.asarray(mask_BxSxS2_ik0).transpose(1, 0, 2),
        "rope": rope_table(),
        "wq": tiled(np.asarray(L0_xattn_Wq), KV * GH).reshape(KV * GH * P, C * D),
        "wk": tiled(np.asarray(L0_xattn_Wk), KV),
        "wv": L0_xattn_Wv,
        "wo": L0_xattn_Wo,
        "router": L0_ffn_router_weight,
        "router_bias": L0_ffn_router_bias,
        "expert_bias": L0_ffn_expert_bias,
    }
    arrays = {f"in_{k}": np.ascontiguousarray(v) for k, v in arrays.items()}
    nc = bacc.Bacc("TRN2", target_bir_lowering=False, num_devices=1)
    ins = [nc.dram_tensor(k, a.shape, mybir.dt.from_np(a.dtype), kind="ExternalInput").ap() for k, a in arrays.items()]
    out = nc.dram_tensor("out", (B, S, E), F32, kind="ExternalOutput").ap()
    xattn_ffn(nc, *ins, out)
    return run_bass_kernel_spmd(nc, [arrays], core_ids=[0]).results[0]["out"]
```

```python
from contextlib import ExitStack

import numpy as np

import concourse.bass as bass
from concourse import mybir

F32 = mybir.dt.float32
F32R = mybir.dt.float32r
BF16 = mybir.dt.bfloat16
I32 = mybir.dt.int32
ALU = mybir.AluOpType
ACT = mybir.ActivationFunctionType
X_AXIS = mybir.AxisListType.X

B, S, E = 8, 128, 512
KV, GH, D = 8, 4, 128
NX, TOP = 64, 8
MAX_POS, THETA = 512, 10000.0
EPS = 1e-5
SCALE = float(D) ** -0.5
MASKED = -(2.0**100)

P = 128
W = 512
C = E // P
T = B * S
HALF = D // 2
HB = W // S
NH = T // W
KB = KV // GH
STEPS = KV * B
QT = KV * NH * GH
AHEAD = 7
FIRST = 2

U_CTX = 0
U_TAB = U_CTX + B
U_K = U_TAB + 2 * NH
U_V = U_K + KV * NH
U_Q = U_V + KB * B
X_AFTER = 5

RA, RB = 2, 4
A_Q = KV
B_O = KB * C
WK = 4


def xattn_ffn(nc, x, ctx, pos, mask, rope, wq, wk, wv, wo, router, router_bias, expert_bias, out):
    with ExitStack() as stack:
        kib = 1024
        base = -(-nc.sbuf_base // 32) * 32

        def at(name, cols, dt, offset, parts=P):
            return nc.alloc_sbuf_tensor_at(name, [parts] + cols, dt, offset=base + int(offset * kib))

        def bank(name):
            return stack.enter_context(nc.psum_tensor(name, [P, W], F32))

        def sem(name):
            return stack.enter_context(nc.semaphore(name))

        xT_hi = at("xT_hi", [C, T], F32R, 0)
        xT_lo = at("xT_lo", [C, T], F32R, 16)
        resid = at("resid", [B, E], F32, 32)
        cosT = at("cosT", [T], F32, 48)
        sinT = at("sinT", [T], F32, 52)
        mask_bias = at("mask_bias", [B, S], BF16, 56)
        kT = at("kT", [KV, T], F32, 58)
        values = at("values", [B, KV * D], F32, 90)
        table = at("table", [B, 2 * D], F32, 90)
        mask_in = at("mask_in", [B, S], I32, 98)
        router_in = at("router_in", [E], F32, 106, NX)
        ctx_in = at("ctx_in", [B, E], F32, 74)
        ff_x = at("ff_x", [3, E], F32, 58)
        ff_xT = at("ff_xT", [E], F32, 64)
        ff_out = at("ff_out", [2, E], F32, 66)
        ff_logit = at("ff_logit", [NX], F32, 70)
        ff_exp = at("ff_exp", [NX], F32, 70.25)
        ff_prob = at("ff_prob", [NX], F32, 70.5)
        ff_rest = at("ff_rest", [NX], F32, 70.75)
        ff_kept = at("ff_kept", [NX], F32, 71)
        ff_keptT = at("ff_keptT", [S], F32, 71.5, NX)
        wv_hi = [at("wv0_hi", [C, W], F32R, 122), at("wv1_hi", [C, W], F32R, 138)]
        wv_lo = [at("wv0_lo", [C, W], F32R, 130), at("wv1_lo", [C, W], F32R, 146)]
        wq_hi = at("wq_hi", [GH, C, D], F32R, 122)
        wq_lo = at("wq_lo", [GH, C, D], F32R, 130)
        wk_hi = at("wk_hi", [WK, C, D], F32R, 138)
        wk_lo = at("wk_lo", [WK, C, D], F32R, 146)
        qT = at("qT", [2, GH, W], F32, 138)
        ctxT_hi = at("ctxT_hi", [C, T], F32R, 154)
        ctxT_lo = at("ctxT_lo", [C, T], F32R, 170)
        wo_hi = at("wo_hi", [GH, E], F32R, 154)
        wo_lo = at("wo_lo", [GH, E], F32R, 162)
        probs = at("probs", [2, GH, S], F32, 170)
        pT_hi = at("pT_hi", [W], F32R, 174)
        pT_lo = at("pT_lo", [W], F32R, 176)
        oT_hi = at("oT_hi", [W], F32R, 178)
        oT_lo = at("oT_lo", [W], F32R, 180)
        v_hi = at("v_hi", [2, D], F32R, 182)
        v_lo = at("v_lo", [2, D], F32R, 183)
        ring_a = at("ring_a", [RA, W], F32, 186)
        ring_b = at("ring_b", [RB, W], F32, 190)
        rot = at("rot", [2, W], F32, 198)
        x_norm = at("x_norm", [2, E], F32, 198)
        ident = at("ident", [P], F32, 202)
        routerT = at("routerT", [C, NX], F32, 202.5)
        ebias = at("ebias", [E], F32, 203.5, NX)
        rbias = at("rbias", [NX], F32, 205.5)
        pos_in = at("pos_in", [B], I32, 205.75)
        pos_wrap = at("pos_wrap", [B], F32, 205.8125)
        pos_sum = at("pos_sum", [B], F32, 205.875)
        pos_idx = at("pos_idx", [B], I32, 205.9375)
        x_stats = at("x_stats", [B, 6], F32, 206)
        x_mv = at("x_mv", [B, 2], F32, 206.1875)
        x_var = at("x_var", [B], F32, 206.25)
        x_rstd = at("x_rstd", [B], F32, 206.28125)
        power = at("power", [B], F32, 206.3125)
        negmax = at("negmax", [2, GH], F32, 206.34375)
        sums = at("sums", [2, GH], F32, 206.375)
        rsum = at("rsum", [2, GH], F32, 206.40625)
        ff_stats = at("ff_stats", [6], F32, 206.4375)
        ff_mv = at("ff_mv", [2, 2], F32, 206.46875)
        ff_var = at("ff_var", [1], F32, 206.5)
        ff_rstd = at("ff_rstd", [2], F32, 206.53125)
        ff_negmax = at("ff_negmax", [1], F32, 206.5625)
        ff_sum = at("ff_sum", [1], F32, 206.59375)
        ff_rsum = at("ff_rsum", [1], F32, 206.625)
        ff_top = at("ff_top", [TOP], F32, 206.65625)
        ff_wsum = at("ff_wsum", [1], F32, 206.6875)
        assert base + int(206.75 * kib) <= nc.sbuf_usable_end

        proj = [bank("proj0"), bank("proj1")]
        score = [bank("score0"), bank("score1")]
        probT = bank("probT")
        attnT = bank("attnT")
        outp = [bank("outp0"), bank("outp1")]
        x_bank = [probT, attnT]

        dma_a = [sem(f"dma_a{i}") for i in range(RA)]
        dma_b = [sem(f"dma_b{i}") for i in range(RB)]
        dma_x = [sem(f"dma_x{i}") for i in range(NH)]
        dma_ctx = [sem(f"dma_ctx{i}") for i in range(B // 2)]
        dma_pos = sem("dma_pos")
        dma_mask = sem("dma_mask")
        dma_table = [sem(f"dma_table{i}") for i in range(B)]
        dma_router = sem("dma_router")
        dma_ffn = sem("dma_ffn")
        dma_out = [sem("dma_out0"), sem("dma_out1")]
        ident_done = sem("ident_done")
        power_done = sem("power_done")
        pos_wrapped = sem("pos_wrapped")
        pos_summed = sem("pos_summed")
        pos_done = sem("pos_done")
        x_counted = sem("x_counted")
        x_averaged = sem("x_averaged")
        var_done = sem("var_done")
        rstd_done = sem("rstd_done")
        norm_done = sem("norm_done")
        router_ps = sem("router_ps")
        router_done = sem("router_done")
        proj_done = sem("proj_done")
        ctx_hi = sem("ctx_hi")
        x_ps = sem("x_ps")
        x_hi = sem("x_hi")
        x_lo = sem("x_lo")
        proj_free = sem("proj_free")
        rot_done = sem("rot_done")
        sin_done = sem("sin_done")
        rope_done = sem("rope_done")
        a_hi = sem("a_hi")
        a_lo = sem("a_lo")
        b_hi = sem("b_hi")
        b_lo = sem("b_lo")
        qk_done = sem("qk_done")
        masked = sem("masked")
        max_done = sem("max_done")
        exp_done = sem("exp_done")
        rsum_done = sem("rsum_done")
        soft_done = sem("soft_done")
        pt_done = sem("pt_done")
        pt_hi = sem("pt_hi")
        pt_lo = sem("pt_lo")
        vhi_done = sem("vhi_done")
        vlo_done = sem("vlo_done")
        pv_done = sem("pv_done")
        ot_hi = sem("ot_hi")
        ot_lo = sem("ot_lo")
        o_done = sem("o_done")
        acc_done = sem("acc_done")
        f_stats = sem("f_stats")
        f_mv = sem("f_mv")
        f_var = sem("f_var")
        f_rstd = sem("f_rstd")
        f_x = sem("f_x")
        f_xT = sem("f_xT")
        f_xTs = sem("f_xTs")
        f_logit = sem("f_logit")
        f_biased = sem("f_biased")
        f_max = sem("f_max")
        f_exp = sem("f_exp")
        f_rsum = sem("f_rsum")
        f_prob = sem("f_prob")
        f_top = sem("f_top")
        f_rest = sem("f_rest")
        f_kept = sem("f_kept")
        f_wsum = sem("f_wsum")
        f_keptT = sem("f_keptT")
        f_keptTs = sem("f_keptTs")
        f_mix = sem("f_mix")
        f_mixed = sem("f_mixed")
        f_out = sem("f_out")

        block = stack.enter_context(nc.Block())

        def wait_ring(eng, sems, r, ring):
            r0, g, per = r if isinstance(r, tuple) else (r, 0, 0)
            eng.wait_ge(sems[r0 % ring], 16 * (r0 // ring + 1) + g * (16 * per // ring))

        def heads(tile):
            return tile.rearrange("p (h k) -> p h k", h=GH)

        def chunks(tile):
            return tile.rearrange("p (c k) -> p c k", c=C)

        @block.sync
        def _(sp):
            def load_wo(g, h):
                sp.wait_ge(b_lo, B_O - RB + h + 1 + g * GH)
                sp.dma_start(ring_b[:, h, :], wo[bass.ds(g * (GH * D) + h * D, D), :]).then_inc(dma_b[h % RB], 16)

            def load_wq(g, h):
                sp.wait_ge(a_lo, A_Q - RA + h + 1 + g * GH)
                sp.dma_start(ring_a[:, h % RA, :], wq[bass.ds(g * (GH * P) + h * P, P), :]).then_inc(dma_a[h % RA], 16)

            def load_wv(i):
                half, c = i // C, i % C
                sp.dma_start(ring_b[:, i % RB, :], wv[c * P:(c + 1) * P, half * W:(half + 1) * W]).then_inc(dma_b[i % RB], 16)

            for i in range(B // 2):
                sp.dma_start(ctx_in[:, 2 * i:2 * i + 2, :], ctx[2 * i:2 * i + 2].rearrange("b s e -> s b e")).then_inc(dma_ctx[i], 16)
                if i < RA:
                    sp.dma_start(ring_a[:, i, :], wk[i]).then_inc(dma_a[i], 16)
            for r in range(RA, KV):
                sp.wait_ge(a_lo, r - RA + 1)
                sp.dma_start(ring_a[:, r % RA, :], wk[r]).then_inc(dma_a[r % RA], 16)
                if r == RA:
                    for half in range(NH):
                        rows = slice(half * HB, (half + 1) * HB)
                        sp.dma_start(resid[:, rows, :], x[rows].rearrange("b s e -> s b e")).then_inc(dma_x[half], 16)
                    for i in range(RB):
                        load_wv(i)
            for i in range(RB, KB * C):
                sp.wait_ge(b_lo, i - RB + 1)
                load_wv(i)
            load_wq(0, 0)
            load_wq(0, 1)
            for h in range(GH):
                load_wo(0, h)
            load_wq(0, 2)
            load_wq(0, 3)
            load_wq(1, 0)
            load_wq(1, 1)

            def stream(g):
                for h in range(GH):
                    load_wo(g + 1, h)
                load_wq(g + 1, 2)
                load_wq(g + 1, 3)

            with sp.Fori(0, KV - 2) as g:
                stream(g)
                load_wq(g + 2, 0)
                load_wq(g + 2, 1)
            stream(KV - 2)
            for b in range(B):
                sp.wait_ge(f_out, b + 1)
                sp.dma_start(out[b], ff_out[:, b % 2, :]).then_inc(dma_out[b % 2], 16)
            for stored in dma_out:
                sp.wait_ge(stored, 16 * B // 2)

        @block.gpsimd
        def _(pool):
            def rotate(k, half):
                k0, g, per = k
                pool.wait_ge(rot_done, k0 + 1 + g * per)
                pool.tensor_tensor(rot[:, k0 % 2, :], rot[:, k0 % 2, :], sinT[:, half * W:(half + 1) * W],
                                   ALU.mult).then_inc(sin_done, 1)

            def lo_a(dst, hi, slot, count):
                pool.wait_ge(a_hi, count)
                pool.tensor_tensor(dst, chunks(ring_a[:, slot, :]), hi.bitcast(F32), ALU.subtract).then_inc(a_lo, 1)

            def lo_b(dst, hi, slot, count):
                pool.wait_ge(b_hi, count)
                pool.tensor_tensor(dst, ring_b[:, slot, :], hi.bitcast(F32), ALU.subtract).then_inc(b_lo, 1)

            pool.memset(ident[:, :], 0.0).then_inc(ident_done, 1)
            pool.memset(power[:, :], -0.5).then_inc(power_done, 1)
            pool.wait_ge(ident_done, 1)
            pool.affine_select(out=ident[:, :], in_=ident[:, :], compare_op=ALU.not_equal, fill=1.0, base=0,
                               pattern=[[-1, P]], channel_multiplier=1).then_inc(ident_done, 1)
            pool.wait_ge(pos_done, 1)
            for b in range(B):
                pool.indirect_dma_start(table[:, b, :], None, rope,
                                        bass.IndirectOffsetOnAxis(ap=pos_idx[:, b:b + 1], axis=0),
                                        bounds_check=MAX_POS - 1).then_inc(dma_table[b], 16)
            for g in range(2):
                lo_a(wk_lo[:, g % WK], wk_hi[:, g % WK], g % RA, g + 1)
            for g in range(KV):
                for half in range(NH):
                    if g == 0 and half == 0:
                        pool.wait_ge(proj_free, U_TAB + 2 * NH)
                    rotate((g * NH + half, 0, 0), half)
                if g + 2 < KV:
                    lo_a(wk_lo[:, (g + 2) % WK], wk_hi[:, (g + 2) % WK], g % RA, g + 3)
                if 3 <= g < 3 + C:
                    i = g - 3
                    lo_b(wv_lo[0][:, i, :], wv_hi[0][:, i, :], i % RB, i + 1)
            pool.wait_ge(power_done, 1)
            pool.wait_ge(var_done, 1)
            pool.tensor_tensor(x_rstd[:, :], x_var[:, :], power[:, :], ALU.pow).then_inc(rstd_done, 1)
            for i in range(C, 2 * C):
                lo_b(wv_lo[1][:, i - C, :], wv_hi[1][:, i - C, :], i % RB, i + 1)
            for h in range(GH):
                lo_a(wq_lo[:, h], wq_hi[:, h], h % RA, A_Q + h + 1)

            def soften(p, count):
                pool.wait_ge(rsum_done, count)
                pool.tensor_tensor(probs[:, p], probs[:, p], rsum[:, p, :].unsqueeze(2).broadcast_to([P, GH, S]),
                                   ALU.mult).then_inc(soft_done, 1)

            for j in range(AHEAD - 1):
                rotate((KV * NH + j, 0, 0), j // GH % NH)
                if j >= GH:
                    soften(j - GH, j - GH + 1)

            def step(g, b, last=False):
                if not (last and b + AHEAD - 1 >= B):
                    rotate((KV * NH + AHEAD - 1 + b, g, B), (b + AHEAD - 1) // GH % NH)
                if b < GH and not last:
                    lo_a(wq_lo[:, b], wq_hi[:, b], b % RA, A_Q + GH + b + 1 + g * GH)
                if b == 0:
                    for h in range(GH):
                        lo_b(wo_lo[:, h, :], wo_hi[:, h, :], h, KB * C + h + 1 + g * GH)
                if not (last and b + FIRST >= B):
                    soften(b % 2, b + FIRST + 1 + g * B)
                if last:
                    ffn(b)

            def ffn(b):
                if 1 <= b < B + 1:
                    ffn_rstd(b - 1)
                if 3 <= b < B + 3:
                    ffn_out(b - 3)

            def ffn_out(b):
                pool.wait_ge(f_mixed, b + 1)
                pool.tensor_tensor(ff_out[:, b % 2, :], ff_out[:, b % 2, :], resid[:, b, :], ALU.add).then_inc(f_out, 1)

            def ffn_rstd(b):
                pool.wait_ge(f_var, b + 1)
                if b >= 2:
                    pool.wait_ge(f_x, b - 1)
                pool.tensor_tensor(ff_rstd[:, b % 2:b % 2 + 1], ff_var[:, :], power[:, 0:1], ALU.pow).then_inc(f_rstd, 1)

            with pool.Fori(0, KV - 1) as g:
                for b in range(B):
                    step(g, b)
            for b in range(B):
                step(KV - 1, b, last=True)
            for b in range(B, B + 3):
                ffn(b)

        @block.scalar
        def _(act):
            def swap_halves(u, k, done_before=True):
                u0, k0, g, per = u[0], k, u[1], u[2]
                act.wait_ge(proj_done, u0 + 1 + g * per)
                if k0 >= 2:
                    act.wait_ge(rope_done, k0 - 1 + g * per)
                act.activation(rot[0:HALF, k0 % 2, :], proj[u0 % 2][HALF:P, :], ACT.Copy)
                act.activation(rot[HALF:P, k0 % 2, :], proj[u0 % 2][0:HALF, :], ACT.Copy).then_inc(rot_done, 1)

            def hi_a(dst, slot):
                act.activation(dst, chunks(ring_a[:, slot, :]), ACT.Copy).then_inc(a_hi, 1)

            def hi_b(dst, slot):
                act.activation(dst, ring_b[:, slot, :], ACT.Copy).then_inc(b_hi, 1)

            def hi_x(b):
                act.wait_ge(x_ps, b + 1)
                act.activation(xT_hi[:, :, b * S:(b + 1) * S], chunks(x_bank[b % 2][:, :]), ACT.Copy).then_inc(x_hi, 1)

            act.dma_start(pos_in[:, :], pos).then_inc(dma_pos, 16)
            act.dma_start(mask_in[:, :, :], mask).then_inc(dma_mask, 16)
            act.dma_start(router_in[:, :], router).then_inc(dma_router, 16)
            act.dma_start(ebias[:, :], expert_bias).then_inc(dma_ffn, 16)
            act.dma_start(rbias[:, :], router_bias.partition_broadcast(P)).then_inc(dma_ffn, 16)
            for b in range(B):
                act.wait_ge(proj_done, U_CTX + b + 1)
                act.activation(ctxT_hi[:, :, b * S:(b + 1) * S], chunks(proj[b % 2][:, :]), ACT.Copy).then_inc(ctx_hi, 1)
            for g in range(2):
                wait_ring(act, dma_a, g, RA)
                hi_a(wk_hi[:, g % WK], g % RA)
            for g in range(KV):
                for half in range(NH):
                    k = g * NH + half
                    swap_halves((U_K + k, 0, 0), k)
                if g + 2 < KV:
                    wait_ring(act, dma_a, g + 2, RA)
                    hi_a(wk_hi[:, (g + 2) % WK], g % RA)
                if 3 <= g < 3 + C:
                    i = g - 3
                    wait_ring(act, dma_b, i, RB)
                    hi_b(wv_hi[0][:, i, :], i % RB)

            for i in range(C, 2 * C):
                wait_ring(act, dma_b, i, RB)
                hi_b(wv_hi[1][:, i - C, :], i % RB)
            for b in range(B - GH):
                hi_x(b)
            act.wait_ge(proj_done, U_V + B)
            for h in range(GH):
                wait_ring(act, dma_a, A_Q + h, RA)
                hi_a(wq_hi[:, h], h % RA)
                hi_x(B - GH + h)

            def exps(p, count, first=False):
                act.wait_ge(max_done, count)
                if not first:
                    act.wait_ge(pt_done, count - FIRST)
                for h in range(GH):
                    last = act.activation(probs[:, p, h, :], heads(score[p][:, :])[:, h, :], ACT.Exp,
                                          bias=negmax[:, p, h:h + 1], accum_out=sums[:, p, h:h + 1])
                last.then_inc(exp_done, 1)

            for j in range(AHEAD - 1):
                swap_halves((U_Q + j, 0, 0), KV * NH + j)
                if j >= GH:
                    exps(j - GH, j - GH + 1, True)

            def step(g, b, first=False, last=False):
                n = b + g * B
                if not (last and b + AHEAD - 1 >= B):
                    swap_halves((U_Q + AHEAD - 1 + b, g, B), KV * NH + AHEAD - 1 + b)
                if not (first and b < 2):
                    act.wait_ge(pv_done, n - 1)
                act.activation(v_hi[:, b % 2, :], values[:, b, bass.ds(g * D, D)], ACT.Copy).then_inc(vhi_done, 1)
                act.wait_ge(pt_done, n + 1)
                if not (first and b == 0):
                    act.wait_ge(pv_done, n)
                act.activation(pT_hi[:, :], probT[:, :], ACT.Copy).then_inc(pt_hi, 1)

                def hi_wo(h):
                    wait_ring(act, dma_b, (B_O + h, g, GH), RB)
                    if not first:
                        act.wait_ge(o_done, n * GH - GH + h + 1)
                    hi_b(wo_hi[:, h, :], h)

                if b < GH and not last:
                    wait_ring(act, dma_a, (A_Q + GH + b, g, GH), RA)
                    act.wait_ge(proj_done, U_Q + GH + b + 1 + g * B)
                    hi_a(wq_hi[:, b], b % RA)
                if b == 0:
                    for h in range(GH):
                        hi_wo(h)
                if not (last and b + FIRST >= B):
                    exps(b % 2, n + FIRST + 1)
                if last:
                    ffn(b, 0)
                act.wait_ge(pv_done, n + 1)
                if not (first and b == 0):
                    act.wait_ge(o_done, n * GH)
                act.activation(oT_hi[:, :], attnT[:, :], ACT.Copy).then_inc(ot_hi, 1)
                if last:
                    ffn(b, 1)

            def ffn(b, part):
                if part == 0 and 2 <= b < B + 2:
                    ffn_xT(b - 2)
                if part == 0 and 3 <= b < B + 3:
                    ffn_kept(b - 3)
                if part == 1 and 2 <= b < B + 2:
                    ffn_exp(b - 2)

            def ffn_xT(b):
                act.wait_ge(f_xT, b + 1)
                if b >= 1:
                    act.wait_ge(f_logit, b)
                act.activation(ff_xT[:, :], proj[0][:, :], ACT.Copy).then_inc(f_xTs, 1)

            def ffn_exp(b):
                act.wait_ge(f_max, b + 1)
                if b >= 1:
                    act.wait_ge(f_prob, b)
                act.activation(ff_exp[:, :], ff_logit[:, :], ACT.Exp, bias=ff_negmax[:, :],
                               accum_out=ff_sum[:, :]).then_inc(f_exp, 1)

            def ffn_kept(b):
                act.wait_ge(f_keptT, b + 1)
                if b >= 1:
                    act.wait_ge(f_mix, b)
                act.activation(ff_keptT[:, :], proj[1][0:NX, 0:S], ACT.Copy).then_inc(f_keptTs, 1)

            for b in range(B):
                step(0, b, first=True)
            with act.Fori(1, KV - 1) as g:
                for b in range(B):
                    step(g, b)
            for b in range(B):
                step(KV - 1, b, last=True)
            for b in range(B, B + 3):
                ffn(b, 0)
                ffn(b, 1)

        @block.vector
        def _(dve):
            def times_cos(u, k, g, per, dst, half):
                dve.wait_ge(rot_done, k + 1 + g * per)
                dve.tensor_tensor(dst, proj[u % 2][:, :], cosT[:, half * W:(half + 1) * W],
                                  ALU.mult).then_inc(proj_free, 1)

            def add_rotated(u, k, g, per, dst):
                dve.wait_ge(sin_done, k + 1 + g * per)
                dve.wait_ge(proj_free, u + 1 + g * per)
                dve.tensor_tensor(dst, dst, rot[:, k % 2, :], ALU.add).then_inc(rope_done, 1)

            dve.wait_ge(dma_pos, 16)
            dve.tensor_scalar(pos_wrap[:, :], pos_in[:, :], 0.0, float(MAX_POS), ALU.is_lt, ALU.mult).then_inc(pos_wrapped, 1)
            dve.wait_ge(pos_wrapped, 1)
            dve.tensor_tensor(pos_sum[:, :], pos_in[:, :], pos_wrap[:, :], ALU.add).then_inc(pos_summed, 1)
            dve.wait_ge(pos_summed, 1)
            dve.tensor_scalar(pos_idx[:, :], pos_sum[:, :], 0.0, float(MAX_POS - 1), ALU.max, ALU.min).then_inc(pos_done, 1)
            for b in range(B):
                rows = slice(b * S, (b + 1) * S)
                dve.wait_ge(ctx_hi, b + 1)
                dve.tensor_tensor(ctxT_lo[:, :, rows], chunks(proj[b % 2][:, :]), ctxT_hi[:, :, rows].bitcast(F32),
                                  ALU.subtract).then_inc(proj_free, 1)
            for i in range(2 * NH):
                u = U_TAB + i
                dve.wait_ge(proj_done, u + 1)
                dst = (cosT, sinT)[i // NH]
                dve.tensor_copy(dst[:, i % NH * W:(i % NH + 1) * W], proj[u % 2][:, :]).then_inc(proj_free, 1)
            dve.wait_ge(router_ps, 1)
            dve.tensor_copy(routerT[:, :, :], score[0][:, 0:C * NX].rearrange("p (c k) -> p c k", c=C)).then_inc(router_done, 1)
            dve.wait_ge(dma_mask, 16)
            dve.tensor_scalar(mask_bias[:, :, :], mask_in[:, :, :], 0.0, MASKED, ALU.is_equal, ALU.mult).then_inc(router_done, 1)
            for g in range(KV):
                for half in range(NH):
                    k = g * NH + half
                    dst = kT[:, g, half * W:(half + 1) * W]
                    times_cos(U_K + k, k, 0, 0, dst, half)
                    add_rotated(U_K + k, k, 0, 0, dst)
                if g % HB == 0:
                    dve.wait_ge(dma_x[g // HB], 16)
                dve.bn_stats(x_stats[:, g, :], resid[:, g, :]).then_inc(x_counted, 1)
            dve.wait_ge(x_counted, B)
            for b in range(B):
                dve.bn_aggr(x_mv[:, b, :], x_stats[:, b, :]).then_inc(x_averaged, 1)
            dve.wait_ge(x_averaged, B)
            dve.tensor_scalar(x_var[:, :], x_mv[:, :, 1], EPS, None, ALU.add).then_inc(var_done, 1)

            def copy_values(i):
                half, b = i // B, i % B
                dve.wait_ge(proj_done, U_V + i + 1)
                dve.tensor_copy(values[:, b, half * W:(half + 1) * W], proj[i % 2][:, :]).then_inc(proj_free, 1)

            def normalise_x(b):
                if b >= 2:
                    dve.wait_ge(x_ps, b - 1)
                dve.tensor_scalar(x_norm[:, b % 2, :], resid[:, b, :], x_mv[:, b, 0:1], x_rstd[:, b:b + 1],
                                  ALU.subtract, ALU.mult).then_inc(norm_done, 1)

            def lo_x(b):
                rows = slice(b * S, (b + 1) * S)
                dve.wait_ge(x_hi, b + 1)
                dve.tensor_tensor(xT_lo[:, :, rows], chunks(x_bank[b % 2][:, :]), xT_hi[:, :, rows].bitcast(F32),
                                  ALU.subtract).then_inc(x_lo, 1)

            for i in range(KB * B):
                copy_values(i)
                if i == 0:
                    dve.wait_ge(rope_done, KV * NH)
                    dve.wait_ge(rstd_done, 1)
                if 0 <= i - X_AFTER + 2 < B:
                    normalise_x(i - X_AFTER + 2)
                if 0 <= i - X_AFTER - 1 < B:
                    lo_x(i - X_AFTER - 1)

            def rope_query(b0, g, part):
                j = b0
                half = j // GH
                dst = qT[:, half % 2, j % GH, :]
                if part == 0:
                    times_cos(U_Q + j, KV * NH + j, g, B, dst, half % NH)
                else:
                    add_rotated(U_Q + j, KV * NH + j, g, B, dst)

            def mask_scores(p, b, count):
                dve.wait_ge(qk_done, count)
                dve.scalar_tensor_tensor(heads(score[p][:, :]), heads(score[p][:, :]), SCALE,
                                         mask_bias[:, b, :].unsqueeze(1).broadcast_to([P, GH, S]),
                                         ALU.mult, ALU.add).then_inc(masked, 1)

            def row_max(p, count, first=False):
                dve.wait_ge(masked, count)
                if not first:
                    dve.wait_ge(exp_done, count - 2)
                dve.tensor_reduce(negmax[:, p, :], heads(score[p][:, :]), X_AXIS, ALU.max, negate=True).then_inc(max_done, 1)

            def invert_sums(p, count, first=False):
                dve.wait_ge(exp_done, count)
                if not first:
                    dve.wait_ge(soft_done, count - 2)
                dve.reciprocal(rsum[:, p, :], sums[:, p, :]).then_inc(rsum_done, 1)

            for j in range(AHEAD - 1):
                rope_query(j, 0, 0)
                rope_query(j, 0, 1)
                if j >= GH:
                    n = j - GH
                    mask_scores(n, n, n + 1)
                    row_max(n, n + 1, True)
                    invert_sums(n, n + 1, True)

            def accumulate(b, count, first):
                dve.wait_ge(o_done, count * GH)
                if not first:
                    dve.wait_ge(acc_done, count - B)
                dve.tensor_tensor(resid[:, b, :], resid[:, b, :], outp[b % 2][:, :], ALU.add).then_inc(acc_done, 1)

            def step(g, b, first=False, last=False):
                n = b + g * B
                ahead = not (last and b + FIRST >= B)
                if ahead:
                    mask_scores(b % 2, (b + FIRST) % B, n + FIRST + 1)
                query = not (last and b + AHEAD - 1 >= B)
                if last:
                    ffn(b, 0)
                if query:
                    if not (first and b + AHEAD - 1 < 2 * GH):
                        dve.wait_ge(qk_done, ((b + AHEAD - 1) // GH - 1) * GH + g * B)
                    rope_query(b + AHEAD - 1, g, 0)
                dve.wait_ge(vhi_done, n + 1)
                if not (first and b < 2):
                    dve.wait_ge(pv_done, n - 1)
                dve.tensor_tensor(v_lo[:, b % 2, :], values[:, b, bass.ds(g * D, D)], v_hi[:, b % 2, :].bitcast(F32),
                                  ALU.subtract).then_inc(vlo_done, 1)
                dve.wait_ge(pt_hi, n + 1)
                if not (first and b == 0):
                    dve.wait_ge(pv_done, n)
                dve.tensor_tensor(pT_lo[:, :], probT[:, :], pT_hi[:, :].bitcast(F32), ALU.subtract).then_inc(pt_lo, 1)
                if ahead:
                    row_max(b % 2, n + FIRST + 1)
                if query:
                    rope_query(b + AHEAD - 1, g, 1)
                if not (first and b == 0):
                    accumulate((b - 1) % B, n, first)
                if last:
                    ffn(b, 1)
                if ahead:
                    invert_sums(b % 2, n + FIRST + 1)
                dve.wait_ge(ot_hi, n + 1)
                if not (first and b == 0):
                    dve.wait_ge(o_done, n * GH)
                dve.tensor_tensor(oT_lo[:, :], attnT[:, :], oT_hi[:, :].bitcast(F32), ALU.subtract).then_inc(ot_lo, 1)
                if last:
                    ffn(b, 2)

            def ffn(b, part):
                if part == 0 and 2 <= b < B + 2:
                    ffn_norm(b - 2)
                if part == 0 and 3 <= b < B + 3:
                    ffn_keep(b - 3)
                if part == 1 and 1 <= b < B + 1:
                    ffn_stats(b - 1)
                if part == 2 and 2 <= b < B + 2:
                    ffn_max(b - 2)
                if part == 2 and 3 <= b < B + 3:
                    ffn_scale(b - 3)

            def ffn_stats(b):
                dve.wait_ge(acc_done, B * (KV - 1) + b + 1)
                dve.bn_stats(ff_stats[:, :], resid[:, b, :]).then_inc(f_stats, 1)
                dve.wait_ge(f_stats, b + 1)
                dve.bn_aggr(ff_mv[:, b % 2, :], ff_stats[:, :]).then_inc(f_mv, 1)
                dve.wait_ge(f_mv, b + 1)
                if b >= 1:
                    dve.wait_ge(f_rstd, b)
                dve.tensor_scalar(ff_var[:, :], ff_mv[:, b % 2, 1:2], EPS, None, ALU.add).then_inc(f_var, 1)

            def ffn_norm(b):
                dve.wait_ge(f_rstd, b + 1)
                if b >= 3:
                    dve.wait_ge(f_xT, b - 2)
                    dve.wait_ge(f_mixed, b - 2)
                dve.tensor_scalar(ff_x[:, b % 3, :], resid[:, b, :], ff_mv[:, b % 2, 0:1], ff_rstd[:, b % 2:b % 2 + 1],
                                  ALU.subtract, ALU.mult).then_inc(f_x, 1)

            def ffn_max(b):
                dve.wait_ge(f_logit, b + 1)
                if b == 0:
                    dve.wait_ge(dma_ffn, 32)
                else:
                    dve.wait_ge(f_exp, b)
                dve.tensor_tensor(ff_logit[:, :], proj[0][:, 0:NX], rbias[:, :], ALU.add).then_inc(f_biased, 1)
                dve.wait_ge(f_biased, b + 1)
                dve.tensor_reduce(ff_negmax[:, :], ff_logit[:, :], X_AXIS, ALU.max, negate=True).then_inc(f_max, 1)

            def ffn_keep(b):
                dve.wait_ge(f_exp, b + 1)
                dve.reciprocal(ff_rsum[:, :], ff_sum[:, :]).then_inc(f_rsum, 1)
                dve.wait_ge(f_rsum, b + 1)
                dve.tensor_scalar(ff_prob[:, :], ff_exp[:, :], ff_rsum[:, :], None, ALU.mult).then_inc(f_prob, 1)
                dve.wait_ge(f_prob, b + 1)
                dve.max(ff_top[:, :], ff_prob[:, :]).then_inc(f_top, 1)
                dve.wait_ge(f_top, b + 1)
                dve.match_replace(ff_rest[:, :], ff_top[:, :], ff_prob[:, :], 0.0).then_inc(f_rest, 1)
                dve.tensor_reduce(ff_wsum[:, :], ff_top[:, :], X_AXIS, ALU.add).then_inc(f_wsum, 1)
                dve.wait_ge(f_rest, b + 1)
                if b >= 1:
                    dve.wait_ge(f_keptT, b)
                dve.tensor_tensor(ff_kept[:, :], ff_prob[:, :], ff_rest[:, :], ALU.subtract).then_inc(f_kept, 1)

            def ffn_scale(b):
                dve.wait_ge(f_mix, b + 1)
                dve.wait_ge(f_wsum, b + 1)
                if b >= 2:
                    dve.wait_ge(dma_out[b % 2], 16 * (b // 2))
                dve.scalar_tensor_tensor(ff_out[:, b % 2, :], ff_x[:, b % 3, :], ff_wsum[:, :], proj[1][:, :],
                                         ALU.mult, ALU.add).then_inc(f_mixed, 1)

            for b in range(B):
                step(0, b, first=True)
            with dve.Fori(1, KV - 1) as g:
                for b in range(B):
                    step(g, b)
            for b in range(B):
                step(KV - 1, b, last=True)
            for b in range(B, B + 3):
                ffn(b, 0)
                if b == B:
                    accumulate(B - 1, STEPS, False)
                ffn(b, 1)
                ffn(b, 2)

        @block.tensor
        def _(pe):
            def three(ps, pairs):
                for i, (s_hi, s_lo, m_hi, m_lo) in enumerate(pairs):
                    pe.matmul(ps, s_hi, m_hi, start=i == 0, stop=False)
                    pe.matmul(ps, s_hi, m_lo, start=False, stop=False)
                    last = pe.matmul(ps, s_lo, m_hi, start=False, stop=i == len(pairs) - 1)
                return last

            def bank_free(u):
                if u >= 2:
                    pe.wait_ge(proj_free, u - 1)

            def transposed(u, tile):
                bank_free(u)
                for c in range(C):
                    last = pe.transpose(proj[u % 2][:, c * P:(c + 1) * P], tile[c], ident[:, :])
                last.then_inc(proj_done, 1)

            pe.wait_ge(ident_done, 2)
            for b in range(B):
                pe.wait_ge(dma_ctx[b // 2], 16)
                transposed(U_CTX + b, [ctx_in[:, b, c * P:(c + 1) * P] for c in range(C)])
            for b in range(B):
                pe.wait_ge(dma_table[b], 16)
            for i in range(2 * NH):
                kind, half = i // NH, i % NH
                transposed(U_TAB + i, [table[:, half * HB + b, kind * D:(kind + 1) * D] for b in range(HB)])
            pe.wait_ge(dma_router, 16)
            for c in range(C):
                last = pe.transpose(score[0][:, c * NX:(c + 1) * NX], router_in[:, c * P:(c + 1) * P], ident[0:NX, 0:NX])
            last.then_inc(router_ps, 1)
            for g in range(KV):
                pe.wait_ge(a_lo, g + 1)
                for half in range(NH):
                    u = U_K + g * NH + half
                    bank_free(u)
                    cols = slice(half * W, (half + 1) * W)
                    three(proj[u % 2][:, :], [(wk_hi[:, g % WK, c, :], wk_lo[:, g % WK, c, :],
                                               ctxT_hi[:, c, cols], ctxT_lo[:, c, cols]) for c in range(C)]).then_inc(proj_done, 1)
            for i in range(KB * B):
                half, b = i // B, i % B
                if b == 0:
                    pe.wait_ge(b_lo, (half + 1) * C)
                u = U_V + i
                bank_free(u)
                rows = slice(b * S, (b + 1) * S)
                three(proj[u % 2][:, :], [(ctxT_hi[:, c, rows], ctxT_lo[:, c, rows],
                                           wv_hi[half][:, c, :], wv_lo[half][:, c, :]) for c in range(C)]).then_inc(proj_done, 1)
                t = i - X_AFTER
                if 0 <= t < B:
                    pe.wait_ge(norm_done, t + 1)
                    if t >= 2:
                        pe.wait_ge(x_lo, t - 1)
                    for c in range(C):
                        last = pe.transpose(x_bank[t % 2][:, c * P:(c + 1) * P], x_norm[:, t % 2, c * P:(c + 1) * P], ident[:, :])
                    last.then_inc(x_ps, 1)

            def project_query(b0, g):
                h, half = b0 % GH, b0 // GH % NH
                if half == 0:
                    pe.wait_ge(a_lo, A_Q + b0 // B * GH + h + 1 + g * GH)
                pe.wait_ge(proj_free, U_Q + b0 - 1 + g * B)
                cols = slice(half * W, (half + 1) * W)
                three(proj[b0 % 2][:, :], [(wq_hi[:, h, c, :], wq_lo[:, h, c, :],
                                            xT_hi[:, c, cols], xT_lo[:, c, cols]) for c in range(C)]).then_inc(proj_done, 1)

            def scores(b0, g, first=False):
                p, b = b0 % 2, b0 % B
                half = b0 // HB
                pe.wait_ge(rope_done, KV * NH + (half + 1) * GH + g * B)
                if not first:
                    pe.wait_ge(exp_done, b0 - 1 + g * B)
                for h in range(GH):
                    last = pe.matmul(score[p][:, h * S:(h + 1) * S], qT[:, half % 2, h, b % HB * S:(b % HB + 1) * S],
                                     kT[:, b0 // B + g, b * S:(b + 1) * S], start=True, stop=True)
                last.then_inc(qk_done, 1)

            def step(g, b, first=False, last=False):
                n = b + g * B
                if not (last and b + FIRST >= B):
                    scores(b + FIRST, g)
                pe.wait_ge(soft_done, n + 1)
                if not (first and b == 0):
                    pe.wait_ge(pt_lo, n)
                for h in range(GH):
                    ins = pe.transpose(probT[:, h * S:(h + 1) * S], probs[:, b % 2, h, :], ident[:, :])
                ins.then_inc(pt_done, 1)
                if not (first and b == 0):
                    output((b - 1) % B, n - 1, first and b < 3, b == 1, g)
                if last:
                    ffn(b, 0)
                if first and b == 0:
                    project_query(AHEAD, 0)
                pe.wait_ge(pt_lo, n + 1)
                pe.wait_ge(vlo_done, n + 1)
                if not (first and b == 0):
                    pe.wait_ge(ot_lo, n)
                three(attnT[:, :], [(v_hi[:, b % 2, :], v_lo[:, b % 2, :], pT_hi[:, :], pT_lo[:, :])]).then_inc(pv_done, 1)
                if not (last and b + AHEAD >= B) and not (first and b == 0):
                    project_query(b + AHEAD, g)
                if last:
                    ffn(b, 1)

            def output(b, n, first, fresh, g):
                pe.wait_ge(ot_lo, n + 1)
                if not first:
                    pe.wait_ge(acc_done, n - 1)
                for h in range(GH):
                    if fresh:
                        pe.wait_ge(b_lo, KB * C + h + 1 + g * GH)
                    cols = slice(h * S, (h + 1) * S)
                    w = (wo_hi[:, h, :], wo_lo[:, h, :])
                    pe.matmul(outp[b % 2][:, :], oT_hi[:, cols], w[0], start=h == 0, stop=False)
                    pe.matmul(outp[b % 2][:, :], oT_hi[:, cols], w[1], start=False, stop=False)
                    pe.matmul(outp[b % 2][:, :], oT_lo[:, cols], w[0], start=False, stop=h == GH - 1).then_inc(o_done, 1)

            def ffn(b, part):
                if part == 0 and 3 <= b < B + 3:
                    ffn_kept(b - 3)
                if part == 0 and 2 <= b < B + 2:
                    ffn_xT(b - 2)
                if part == 1 and 2 <= b < B + 2:
                    ffn_logits(b - 2)
                if part == 1 and 3 <= b < B + 3:
                    ffn_mix(b - 3)

            def ffn_xT(b):
                pe.wait_ge(f_x, b + 1)
                if b == 0:
                    pe.wait_ge(proj_free, U_Q + QT - 1)
                else:
                    pe.wait_ge(f_biased, b)
                for c in range(C):
                    last = pe.transpose(proj[0][:, c * P:(c + 1) * P], ff_x[:, b % 3, c * P:(c + 1) * P], ident[:, :])
                last.then_inc(f_xT, 1)

            def ffn_logits(b):
                pe.wait_ge(f_xTs, b + 1)
                for c in range(C):
                    last = pe.matmul(proj[0][:, 0:NX], ff_xT[:, c * P:(c + 1) * P], routerT[:, c, :],
                                     start=c == 0, stop=c == C - 1)
                last.then_inc(f_logit, 1)

            def ffn_kept(b):
                pe.wait_ge(f_kept, b + 1)
                if b == 0:
                    pe.wait_ge(proj_free, U_Q + QT)
                else:
                    pe.wait_ge(f_mixed, b)
                pe.transpose(proj[1][0:NX, 0:S], ff_kept[:, :], ident[:, :]).then_inc(f_keptT, 1)

            def ffn_mix(b):
                pe.wait_ge(f_keptTs, b + 1)
                if b == 0:
                    pe.wait_ge(dma_ffn, 32)
                pe.matmul(proj[1][:, :], ff_keptT[:, :], ebias[:, :], start=True, stop=True).then_inc(f_mix, 1)

            for j in range(AHEAD):
                if j % GH == 0:
                    pe.wait_ge(x_lo, (j // GH + 1) * HB)
                project_query(j, 0)
                if j == GH:
                    pe.wait_ge(router_done, 2)
                if GH <= j < GH + FIRST:
                    scores(j - GH, 0, True)
            for b in range(B):
                step(0, b, first=True)
            with pe.Fori(1, KV - 1) as g:
                for b in range(B):
                    step(g, b)
            for b in range(B):
                step(KV - 1, b, last=True)
            output(B - 1, STEPS - 1, False, False, KV - 1)
            for b in range(B, B + 3):
                ffn(b, 0)
                ffn(b, 1)


def rope_table():
    inv = (np.float32(1.0) / np.float32(THETA) ** (np.arange(0, D, 2, dtype=np.float32) / np.float32(D))).astype(np.float32)
    angle = np.arange(MAX_POS, dtype=np.float32)[:, None] * inv[None, :]
    cos, sin = np.cos(angle), np.sin(angle)
    return np.concatenate([cos, cos, -sin, sin], axis=1).astype(np.float32)


def kernel(x, ctx_4096, pos_BxS2, mask_BxSxS2_ik0, L0_xattn_Wq, L0_xattn_Wk, L0_xattn_Wv, L0_xattn_Wo,
           L0_ffn_router_weight, L0_ffn_router_bias, L0_ffn_expert_bias):
    import concourse.bacc as bacc
    from concourse.bass_utils import run_bass_kernel_spmd

    def tiled(w, n):
        return w.reshape(C, P, n, D).transpose(2, 1, 0, 3).reshape(n, P, C * D)

    arrays = {
        "x": x,
        "ctx": ctx_4096,
        "pos": np.asarray(pos_BxS2).T,
        "mask": np.asarray(mask_BxSxS2_ik0).transpose(1, 0, 2),
        "rope": rope_table(),
        "wq": tiled(np.asarray(L0_xattn_Wq), KV * GH).reshape(KV * GH * P, C * D),
        "wk": tiled(np.asarray(L0_xattn_Wk), KV),
        "wv": L0_xattn_Wv,
        "wo": L0_xattn_Wo,
        "router": L0_ffn_router_weight,
        "router_bias": L0_ffn_router_bias,
        "expert_bias": L0_ffn_expert_bias,
    }
    arrays = {f"in_{k}": np.ascontiguousarray(v) for k, v in arrays.items()}
    nc = bacc.Bacc("TRN2", target_bir_lowering=False, num_devices=1)
    ins = [nc.dram_tensor(k, a.shape, mybir.dt.from_np(a.dtype), kind="ExternalInput").ap() for k, a in arrays.items()]
    out = nc.dram_tensor("out", (B, S, E), F32, kind="ExternalOutput").ap()
    xattn_ffn(nc, *ins, out)
    return run_bass_kernel_spmd(nc, [arrays], core_ids=[0]).results[0]["out"]
```
